# Optimizing a Trainium2 kernel written in Bass

```python
import numpy as np
import jax
import jax.numpy as jnp

def _softmax(x, axis=-1):
    return jax.nn.softmax(x, axis=axis)

def _gelu(x):
    return jax.nn.gelu(x, approximate=True)

def _silu(x):
    return jax.nn.silu(x)

def _sigmoid(x):
    return jax.nn.sigmoid(x)

def _layernorm(x, axis=-1, eps=1e-05):
    m = jnp.mean(x, axis=axis, keepdims=True)
    v = jnp.var(x, axis=axis, keepdims=True)
    return (x - m) / jnp.sqrt(v + eps)

def _scatter_add(tgt, idx, src, axis=0):
    return tgt.at[idx].add(src)

def _segment_sum(src, seg, n):
    return jax.ops.segment_sum(src, seg, n)
kernel_name = 'mk_xattn_ffn_d1_seqx_r4_3d2392'

def setup_inputs(seed: int=0):
    np.random.seed(seed)
    _w = jnp.asarray

    def _rec_inputs():
        import jax
        import jax.numpy as jnp
        _rk = jax.random.key(seed)
        x = -0.0003929 + 0.9999 * jax.random.normal(jax.random.fold_in(_rk, 1), (32, 128, 1024), jnp.float32)
        _lenS = 128 - jax.random.randint(jax.random.fold_in(_rk, 7), (32,), 0, max(1, 128 // 4) + 1, jnp.int32)
        _lenS2 = 128 - jax.random.randint(jax.random.fold_in(_rk, 8), (32,), 0, max(1, 128 // 4) + 1, jnp.int32)
        _ctx_4096P = jax.random.normal(jax.random.fold_in(_rk, 11), (32, 16, 1024), jnp.float32)
        _ctx_4096c = jax.random.dirichlet(jax.random.fold_in(_rk, 511), 0.3 * jnp.ones((16,), jnp.float32), (32, 128))
        _ctx_4096t = jnp.einsum('bsk,bkd->bsd', _ctx_4096c, _ctx_4096P)
        _ctx_4096t = _ctx_4096t * jax.lax.rsqrt(jnp.mean(jnp.square(_ctx_4096t)) + 1e-12) * 0.953939
        ctx_4096 = 2.81802e-05 + 1.00001 * (_ctx_4096t + 0.3 * jax.random.normal(jax.random.fold_in(_rk, 611), (32, 128, 1024), jnp.float32))
        return (x, ctx_4096)
    x, ctx_4096 = _rec_inputs()

    def _L0_xattn_setup():
        import jax, jax.numpy as jnp
        import numpy as np
        HEADS = 8
        DIM_HEAD = 64
        DIM = 128
        HIDDEN = HEADS * DIM_HEAD
        B, N = (8, 1024)
        key = jax.random.key(seed)
        ks = jax.random.split(key, 7)
        s = 0.02
        return {'x': jax.random.normal(ks[0], (B, DIM, N), dtype=jnp.float32), 'context': jax.random.normal(ks[1], (B, DIM, N), dtype=jnp.float32), 'Wq': jax.random.normal(ks[2], (HIDDEN, DIM), dtype=jnp.float32) * s, 'Wkv': jax.random.normal(ks[3], (2 * HIDDEN, DIM), dtype=jnp.float32) * s, 'Wout': jax.random.normal(ks[4], (DIM, HIDDEN), dtype=jnp.float32) * s, 'b_out': jnp.zeros((DIM,), dtype=jnp.float32), 'g': jnp.ones((1, DIM, 1), dtype=jnp.float32)}
    _L0_xattn_all = _L0_xattn_setup()
    _L0_xattn_in = {k: v for k, v in _L0_xattn_all.items() if k in ('Wq', 'Wkv', 'Wout', 'b_out', 'g')}
    del _L0_xattn_all

    def _L0_ffn_setup():
        import jax, jax.numpy as jnp
        import numpy as np
        BATCH, SEQ, D = (2, 512, 1024)
        K, TOPK, RANK = (64, 16, 16)
        ALPHA = 32.0
        SCALING = ALPHA / RANK
        key = jax.random.key(seed)
        k1, k2, k3, k4 = jax.random.split(key, 4)
        x = jax.random.normal(k1, (BATCH, SEQ, D), dtype=jnp.float32)
        A = jax.random.normal(k2, (K, RANK, D), dtype=jnp.float32) * 0.02
        B = jax.random.normal(k3, (K, D, RANK), dtype=jnp.float32) * 0.02
        Wr = jax.random.normal(k4, (K, D), dtype=jnp.float32) * 0.02
        return {'x': x, 'A': A, 'B': B, 'Wr': Wr}
    _L0_ffn_all = _L0_ffn_setup()
    _L0_ffn_in = {k: v for k, v in _L0_ffn_all.items() if k in ('A', 'B', 'Wr')}
    del _L0_ffn_all
    return {'x': x, 'ctx_4096': ctx_4096, 'L0_xattn_Wq': _L0_xattn_in['Wq'], 'L0_xattn_Wkv': _L0_xattn_in['Wkv'], 'L0_xattn_Wout': _L0_xattn_in['Wout'], 'L0_xattn_b_out': _L0_xattn_in['b_out'], 'L0_xattn_g': _L0_xattn_in['g'], 'L0_ffn_A': _L0_ffn_in['A'], 'L0_ffn_B': _L0_ffn_in['B'], 'L0_ffn_Wr': _L0_ffn_in['Wr']}

def reference(x, ctx_4096, L0_xattn_Wq, L0_xattn_Wkv, L0_xattn_Wout, L0_xattn_b_out, L0_xattn_g, L0_ffn_A, L0_ffn_B, L0_ffn_Wr):
    import jax
    import jax.numpy as jnp

    def _L0_xattn_ref(x, context, Wq, Wkv, Wout, b_out, g):
        import jax, jax.numpy as jnp
        import numpy as np
        HEADS = 8
        DIM_HEAD = 64
        DIM = 128
        HIDDEN = HEADS * DIM_HEAD
        B, N = (8, 1024)
        scale = DIM_HEAD ** (-0.5)
        q = jnp.einsum('oc,bcn->bon', Wq, x)
        kv = jnp.einsum('oc,bcn->bon', Wkv, context)
        k, v = jnp.split(kv, 2, axis=1)

        def split_heads(t):
            b, hc, n = t.shape
            return t.reshape(b, HEADS, DIM_HEAD, n)
        q = jax.nn.softmax(split_heads(q), axis=-2) * scale
        k = jax.nn.softmax(split_heads(k), axis=-1)
        v = split_heads(v)
        ctx = jnp.einsum('bhdn,bhen->bhde', k, v)
        out = jnp.einsum('bhde,bhdn->bhen', ctx, q)
        b, h, e, n = out.shape
        out = out.reshape(b, h * e, n)
        out = jnp.einsum('oc,bcn->bon', Wout, out) + b_out[None, :, None]
        mean = jnp.mean(out, axis=1, keepdims=True)
        var = jnp.var(out, axis=1, keepdims=True)
        return (out - mean) * jax.lax.rsqrt(var + 1e-05) * g

    def _L0_ffn_ref(x, A, B, Wr):
        import jax, jax.numpy as jnp
        import numpy as np
        BATCH, SEQ, D = (2, 512, 1024)
        K, TOPK, RANK = (64, 16, 16)
        ALPHA = 32.0
        SCALING = ALPHA / RANK
        prefix = x.shape[:-1]
        xf = x.reshape(-1, x.shape[-1])
        N = xf.shape[0]
        scores = xf @ Wr.T
        top_vals, top_idx = jax.lax.top_k(scores, TOPK)
        gates = jax.nn.softmax(top_vals, axis=-1)
        G = jnp.zeros((N, K), xf.dtype).at[jnp.arange(N)[:, None], top_idx].set(gates)
        h = jnp.einsum('nd,krd->nkr', xf, A)
        out = jnp.einsum('nkr,kdr->nd', h * G[:, :, None], B)
        return (out * SCALING).reshape(*prefix, -1)
    x = x + _L0_xattn_ref(_layernorm(x, axis=-1), ctx_4096, L0_xattn_Wq, L0_xattn_Wkv, L0_xattn_Wout, L0_xattn_b_out, L0_xattn_g)
    x = x + _L0_ffn_ref(_layernorm(x, axis=-1), L0_ffn_A, L0_ffn_B, L0_ffn_Wr)
    return x

_drawn_inputs = setup_inputs


def setup_inputs(seed=0):
    import zlib

    import numpy as np

    out = dict(_drawn_inputs(seed))
    spreads = {'L0_xattn_b_out': (0.0, 0.272), 'L0_xattn_g': (1.0, 0.2)}
    factors = {'ctx_4096': 8.0,
     'L0_xattn_Wq': 8.0,
     'L0_xattn_Wkv': 8.0,
     'L0_xattn_Wout': 8.0,
     'L0_ffn_A': 2.858,
     'L0_ffn_B': 2.694,
     'L0_ffn_Wr': 3.085}
    for name, (base, spread) in spreads.items():
        noise = np.random.default_rng([zlib.crc32(name.encode()), seed]).standard_normal(out[name].shape)
        drawn = base * np.exp(spread * noise) if base else spread * noise
        out[name] = jnp.asarray(drawn.astype(out[name].dtype))
    for name, factor in factors.items():
        out[name] = (out[name] * factor).astype(out[name].dtype)
    return out
```

```python
from contextlib import ExitStack

import concourse.bass as bass
from concourse import mybir

F32 = mybir.dt.float32
F32R = mybir.dt.float32r
ALU = mybir.AluOpType
ACT = mybir.ActivationFunctionType
X = mybir.AxisListType.X

P = 128
BANK = 512
BATCHES, N = 32, 1024
HEADS, DH = 8, 64
HD = HEADS * DH
CH = HD // P
NCH = N // P
EXPERTS, RANK, TOPK = 64, 16, 16
KR = EXPERTS * RANK
KCH = KR // P
EPS = 1e-5
MIX_SCALE = 32.0 / RANK
LOWEST = -3.4028234e38


def wait_for(eng, sem, value):
    if isinstance(value, int) and value <= 0:
        return
    eng.wait_ge(sem, value)


def per_row(col, groups, width):
    return col.unsqueeze(2).broadcast_to([col.shape[0], groups, width])


def split_products(pe, out, stat_hi, stat_lo, mov_hi, mov_lo, first, last):
    pe.matmul(out, stat_hi, mov_hi, start=first, stop=False)
    pe.matmul(out, stat_hi, mov_lo, start=False, stop=False)
    return pe.matmul(out, stat_lo, mov_hi, start=False, stop=last)


def attention_weights(nc, ident, ps, w, Wq, Wkv, Wout, b_out, g):
    with ExitStack() as ctx:
        def sb(name, shape, dt=F32):
            return ctx.enter_context(nc.sbuf_tensor(name, shape, dt))

        def sem(name):
            return ctx.enter_context(nc.semaphore(name))

        wq_raw = sb("wq_raw", [P, CH, P])
        wk_raw = sb("wk_raw", [P, CH, P])
        wv_raw = sb("wv_raw", [P, CH, P])
        wo_raw = sb("wo_raw", [P, HD])
        b_rows = sb("bias_rows", [P, P])
        b_col = sb("b_col", [P, 1])
        b_mean = sb("b_mean", [P, 1])
        wo_sum = sb("wo_sum", [P, CH])
        wo_mean = sb("wo_mean", [P, CH])
        wo_pairs = sb("wo_pairs", [P, CH, 2, P])

        weights_loaded = sem("weights_loaded")
        ident_zeroed = sem("ident_zeroed")
        ident_ready = sem("ident_ready")
        turned = sem("turned")
        wo_step = sem("wo_step")
        b_step = sem("b_step")
        wo_centred = sem("wo_centred")
        hi_ready = sem("hi_ready")
        lo_ready = sem("lo_ready")
        folded = sem("folded")
        qT, kT, oT, z = ps[:, 0, 0], ps[:, 0, 1], ps[:, 1, 0], ps[:, 2]
        block = ctx.enter_context(nc.Block())

        @block.sync
        def _(sp):
            for dst, src in ((wq_raw[:, :, :], Wq.rearrange("(j p) c -> p j c", p=P)),
                             (wk_raw[:, :, :], Wkv[0:HD, :].rearrange("(j p) c -> p j c", p=P)),
                             (wv_raw[:, :, :], Wkv[HD:2 * HD, :].rearrange("(j p) c -> p j c", p=P)),
                             (wo_raw[:, :], Wout),
                             (b_rows[:, :], b_out.rearrange("(a c) -> a c", a=1).broadcast_to([P, P])),
                             (b_col[:, :], b_out.rearrange("(c a) -> c a", a=1)),
                             (w["g"][:, :], g.rearrange("a c b -> (a c) b"))):
                sp.dma_start(dst, src).then_inc(weights_loaded, 16)

        @block.gpsimd
        def _(pool):
            pool.memset(w["minus_half"][:, :], -0.5)
            pool.memset(w["one"][:, :], 1.0)
            pool.memset(ident[:, :], 0.0).then_inc(ident_zeroed, 1)
            pool.wait_ge(ident_zeroed, 1)
            pool.affine_select(out=ident[:, :], in_=ident[:, :], compare_op=ALU.not_equal, fill=1.0,
                               base=0, pattern=[[-1, P]], channel_multiplier=1).then_inc(ident_ready, 1)

        @block.tensor
        def _(pe):
            pe.wait_ge(weights_loaded, 7 * 16)
            pe.wait_ge(ident_ready, 1)
            for j in range(CH):
                pe.transpose(qT[:, j * P:(j + 1) * P], wq_raw[:, j, :], ident[:, :])
            for j in range(CH):
                pe.transpose(kT[:, j * P:(j + 1) * P], wk_raw[:, j, :], ident[:, :])
            for j in range(CH):
                last = pe.transpose(oT[:, j * P:(j + 1) * P], wo_raw[:, j * P:(j + 1) * P], ident[:, :])
            last.then_inc(turned, 1)
            pe.wait_ge(wo_centred, 2)
            for j in range(CH):
                last = pe.matmul(z[:, j // 2, (j % 2) * 2 * P:(j % 2 + 1) * 2 * P], wv_raw[:, j, :],
                                 wo_pairs[:, j, :, :], start=True, stop=True)
            last.then_inc(folded, 1)

        @block.vector
        def _(dve):
            dve.memset(wo_pairs[:, :, :, :], 0.0).then_inc(wo_step, 1)
            dve.wait_ge(weights_loaded, 7 * 16)
            dve.reduce_sum(b_mean[:, :], b_rows[:, :], axis=X).then_inc(b_step, 1)
            dve.wait_ge(b_step, 1)
            dve.tensor_scalar(b_mean[:, :], b_mean[:, :], 1.0 / P, None, ALU.mult).then_inc(b_step, 1)
            dve.wait_ge(b_step, 2)
            dve.tensor_tensor(w["bias"][:, :], b_col[:, :], b_mean[:, :], ALU.subtract)
            dve.wait_ge(turned, 1)
            oT3 = oT.rearrange("p (j c) -> p j c", j=CH)
            dve.reduce_sum(wo_sum[:, :], oT3, axis=X).then_inc(wo_step, 1)
            dve.wait_ge(wo_step, 2)
            dve.tensor_scalar(wo_mean[:, :], wo_sum[:, :], 1.0 / P, None, ALU.mult).then_inc(wo_step, 1)
            dve.wait_ge(wo_step, 3)
            for h in range(2):
                r = slice(h * DH, (h + 1) * DH)
                dve.tensor_tensor(wo_pairs[r, :, h, :], oT3[r, :, :], per_row(wo_mean[r, :], CH, P),
                                  ALU.subtract).then_inc(wo_centred, 1)
            dve.tensor_copy(w["q_hi"][:, :], qT).then_inc(hi_ready, 1)
            dve.tensor_scalar(w["k_hi"][:, :], kT, -1.0, None, ALU.mult).then_inc(hi_ready, 1)
            dve.wait_ge(hi_ready, 2)
            dve.tensor_tensor(w["q_lo"][:, :], qT, w["q_hi"][:, :].bitcast(F32), ALU.subtract)
            dve.scalar_tensor_tensor(out=w["k_lo"][:, :], in0=kT, scalar=-1.0, in1=w["k_hi"][:, :].bitcast(F32),
                                     op0=ALU.mult, op1=ALU.subtract)
            dve.wait_ge(folded, 1)
            z2 = ps[:, 2].rearrange("p a b -> p (a b)")
            dve.tensor_copy(w["z_hi"][:, :], z2).then_inc(hi_ready, 1)
            dve.wait_ge(hi_ready, 3)
            dve.tensor_tensor(w["z_lo"][:, :], z2, w["z_hi"][:, :].bitcast(F32), ALU.subtract)


RING = ["QT0", "M0", "Q0", "QT1", "K0", "QT2", "Q1", "QT3", "K1",
        "KT0", "Q2", "KT1", "K2", "KT2", "Q3", "KT3", "K3", "C0"]
SLOTS = 3
DELAY = {"K": 0, "C": 0, "Q": 1, "KT": 1, "M": 2, "QT": 2}
PER_BATCH = {"K": 4, "C": 1, "Q": 4, "KT": 4, "M": 1, "QT": 4}
STEPS = BATCHES + 2
FULL_FROM, FULL_TO = 4, BATCHES - 2


def attention(nc, ident, ps, w, x, context, o_dram):
    with ExitStack() as ctx:
        def sb(name, shape, dt=F32):
            return ctx.enter_context(nc.sbuf_tensor(name, shape, dt))

        def sem(name):
            return ctx.enter_context(nc.semaphore(name))

        x_sb = sb("x_sb", [P, 2, N])
        ctx_sb = sb("ctx_sb", [P, 2, N])
        ctx_hi = sb("ctx_hi", [P, 2, N], F32R)
        ctx_lo = sb("ctx_lo", [P, 2, N], F32R)
        xn = sb("xn", [P, N])
        xn_hi = sb("xn_hi", [P, 2, N], F32R)
        xn_lo = sb("xn_lo", [P, 2, N], F32R)
        cT_hi = sb("cT_hi", [P, NCH, P], F32R)
        cT_lo = sb("cT_lo", [P, NCH, P], F32R)
        ek = sb("ek", [P, 2, CH, N])
        eq = sb("eq", [P, 2, NCH, HD])
        kT_hi = sb("kT_hi", [P, 2, 2, HD], F32R)
        kT_lo = sb("kT_lo", [P, 2, 2, HD], F32R)
        q_hi = sb("qh", [P, 2, N], F32R)
        q_lo = sb("ql", [P, 2, N], F32R)
        t_hi = sb("t_hi", [P, HD], F32R)
        t_lo = sb("t_lo", [P, HD], F32R)
        m_full = sb("m_full", [P, CH, P])
        m_hi = sb("m_hi", [P, CH, P], F32R)
        m_lo = sb("m_lo", [P, CH, P], F32R)
        o_sb = sb("o_sb", [P, 2, N])
        k_min = sb("k_min", [P, 2, CH])
        k_sum = sb("k_sum", [P, 3, CH])
        k_inv = sb("k_inv", [P, CH])
        q_max = sb("q_max", [P, 4, 2 * HEADS])
        q_sum = sb("q_sum", [P, 4, 2 * HEADS])
        q_inv = sb("q_inv", [P, 4, 2 * HEADS])
        stats = sb("stats", [P, 2, 6])
        mv = sb("mv", [P, 2])
        veps = sb("veps", [P, 1])
        rstd = sb("rstd", [P, 1])
        shift = sb("shift", [P, 1])

        ctx_loaded = [sem(f"ctx_loaded{i}") for i in range(2)]
        x_loaded = [sem(f"x_loaded{i}") for i in range(2)]
        o_stored = [sem(f"o_stored{i}") for i in range(2)]
        k_made, c_turned, q_made = sem("k_made"), sem("c_turned"), sem("q_made")
        kT_turned, q_turned = sem("kT_turned"), sem("q_turned")
        t_part, m_made, o_part = sem("t_part"), sem("m_made"), sem("o_part")
        k_min_ready, q_max_ready, q_shifted = sem("k_min_ready"), sem("q_max_ready"), sem("q_shifted")
        q_summed, q_inv_ready = sem("q_summed"), sem("q_inv_ready")
        q_lo_ready, kT_lo_ready, cT_lo_ready = sem("q_lo_ready"), sem("kT_lo_ready"), sem("cT_lo_ready")
        t_lo_ready, k_inv_ready, m_scaled, m_lo_ready = (
            sem("t_lo_ready"), sem("k_inv_ready"), sem("m_scaled"), sem("m_lo_ready"))
        x_stats, x_mean_ready, veps_ready, shift_ready = (
            sem("x_stats"), sem("x_mean_ready"), sem("veps_ready"), sem("shift_ready"))
        k_exp, q_exp, q_hi_ready, kT_hi_ready = sem("k_exp"), sem("q_exp"), sem("q_hi_ready"), sem("kT_hi_ready")
        cT_hi_ready, t_hi_ready, m_hi_ready, o_copied = (
            sem("cT_hi_ready"), sem("t_hi_ready"), sem("m_hi_ready"), sem("o_copied"))
        q_normed, ctx_hi_ready, ctx_lo_ready = sem("q_normed"), sem("ctx_hi_ready"), sem("ctx_lo_ready")
        rstd_ready, xn_ready, xn_hi_ready, xn_lo_ready = (
            sem("rstd_ready"), sem("xn_ready"), sem("xn_hi_ready"), sem("xn_lo_ready"))

        slot_read = {"K": k_exp, "C": cT_lo_ready, "Q": q_shifted, "KT": kT_lo_ready, "M": m_scaled,
                     "QT": q_lo_ready}

        def slot(job):
            return ps[:, RING.index(job) % SLOTS]

        def flat(job):
            return slot(job).rearrange("p a b -> p (a b)")

        acc = ps[:, SLOTS]
        acc_flat = acc.rearrange("p a b -> p (a b)")

        def wait_slot(eng, job, s, edge):
            n, back = RING.index(job), 0
            while True:
                n -= SLOTS
                if n < 0:
                    n, back = n + len(RING), back + 1
                kind, i = RING[n][:-1], int(RING[n][-1])
                b = s - back - DELAY[kind]
                if edge and not 0 <= b < BATCHES:
                    if s - back < 0:
                        return
                    continue
                per = PER_BATCH[kind]
                wait_for(eng, slot_read[kind], per * b + i + 1 if kind != "M" else 2 * b + 2)
                return

        def on(kind, s, edge):
            return not edge or 0 <= s - DELAY[kind] < BATCHES

        def each_step(eng, step):
            for s in range(FULL_FROM):
                step(s, s % 2, True)
            with eng.Fori(FULL_FROM // 2, FULL_TO // 2) as i:
                for parity in range(2):
                    step(2 * i + parity, parity, False)
            for s in range(FULL_TO, STEPS):
                step(s, s % 2, True)

        block = ctx.enter_context(nc.Block())

        @block.sync
        def _(sp):
            def step(s, par, edge):
                if not edge or s + 1 < BATCHES:
                    wait_for(sp, ctx_lo_ready, s)
                    wait_for(sp, c_turned, s)
                    sp.dma_start(ctx_sb[:, 1 - par, :], context[s + 1]).then_inc(ctx_loaded[1 - par], 16)
                    wait_for(sp, xn_ready, s)
                    sp.dma_start(x_sb[:, 1 - par, :], x[s + 1]).then_inc(x_loaded[1 - par], 16)
                if on("QT", s, edge):
                    sp.wait_ge(o_copied, s - 2 + 1)
                    sp.dma_start(o_dram[s - 2], o_sb[:, par, :]).then_inc(o_stored[par], 16)

            sp.dma_start(ctx_sb[:, 0, :], context[0]).then_inc(ctx_loaded[0], 16)
            sp.dma_start(x_sb[:, 0, :], x[0]).then_inc(x_loaded[0], 16)
            each_step(sp, step)
            for sem_ in o_stored:
                sp.wait_ge(sem_, 16 * BATCHES // 2)

        @block.gpsimd
        def _(pool):
            def split_context(b, par):
                pool.wait_ge(ctx_loaded[par], 8 * (b - par) + 16)
                wait_for(pool, k_made, CH * (b - 1))
                pool.tensor_tensor(ctx_hi[:, par, :], ctx_sb[:, par, :], w["one"][:, 0:1].broadcast_to([P, N]),
                                   ALU.mult).then_inc(ctx_hi_ready, 1)
                pool.wait_ge(ctx_hi_ready, b + 1)
                pool.tensor_tensor(ctx_lo[:, par, :], ctx_sb[:, par, :], ctx_hi[:, par, :].bitcast(F32),
                                   ALU.subtract).then_inc(ctx_lo_ready, 1)

            def rstd_x(b):
                pool.wait_ge(veps_ready, b + 1)
                wait_for(pool, xn_ready, b)
                pool.tensor_tensor(rstd[:, :], veps[:, :], w["minus_half"][:, :], ALU.pow).then_inc(rstd_ready, 1)

            def split_x(b, par):
                wait_for(pool, q_made, 4 * (b - 1))
                pool.wait_ge(xn_hi_ready, b + 1)
                pool.tensor_tensor(xn_lo[:, par, :], xn[:, :], xn_hi[:, par, :].bitcast(F32),
                                   ALU.subtract).then_inc(xn_lo_ready, 1)

            def norm_queries(b, par, i):
                pool.wait_ge(q_inv_ready, 4 * b + i + 1)
                v = eq[:, par, 2 * i:2 * i + 2, :].rearrange("p n (h d) -> p (n h) d", d=DH)
                pool.tensor_tensor(v, v, per_row(q_inv[:, i, :], 2 * HEADS, DH), ALU.mult).then_inc(q_normed, 1)

            def step(s, par, edge):
                if on("Q", s, edge):
                    norm_queries(s - 1, 1 - par, 0)
                if not edge or s + 1 < BATCHES:
                    split_context(s + 1, 1 - par)
                if on("Q", s, edge):
                    norm_queries(s - 1, 1 - par, 1)
                if on("Q", s, edge):
                    norm_queries(s - 1, 1 - par, 2)
                if on("K", s, edge):
                    rstd_x(s)
                if on("Q", s, edge):
                    norm_queries(s - 1, 1 - par, 3)
                if on("K", s, edge):
                    split_x(s, par)

            split_context(0, 0)
            each_step(pool, step)

        @block.scalar
        def _(act):
            def turned_query(s, par, j):
                b = s - 2
                act.wait_ge(q_turned, 4 * b + j + 1)
                wait_for(act, o_part, 4 * b + j - 1)
                act.copy(q_hi[:, j % 2, :], flat(f"QT{j}")).then_inc(q_hi_ready, 1)

            def turned_keys(s, par, i):
                b = s - 1
                act.wait_ge(kT_turned, 4 * b + i + 1)
                wait_for(act, t_part, 4 * b + i - 1)
                act.copy(kT_hi[:, i % 2, :, :], slot(f"KT{i}")).then_inc(kT_hi_ready, 1)

            def exp_queries(s, par, i):
                b, p = s - 1, 1 - par
                act.wait_ge(q_shifted, 4 * b + i + 1)
                v = eq[:, p, 2 * i:2 * i + 2, :]
                act.activation(v, v, ACT.Exp).then_inc(q_exp, 1)

            def exp_keys(s, par, i, k3):
                act.wait_ge(k_min_ready, 4 * s + i + 1)
                act.activation(ek[:, par, i, :], flat(f"K{i}"), ACT.Exp, bias=k_min[:, par, i:i + 1], scale=-1.0,
                               accum_out=k_sum[:, par, i:i + 1]).then_inc(k_exp, 1)

            def step(s, par, edge):
                QT, M, Q, K, KT, C = (on(k, s, edge) for k in ("QT", "M", "Q", "K", "KT", "C"))
                if QT:
                    turned_query(s, par, 0)
                if M:
                    act.wait_ge(m_scaled, 2 * (s - 2) + 2)
                    wait_for(act, o_part, 4 * (s - 2))
                    act.copy(m_hi[:, :, :], m_full[:, :, :]).then_inc(m_hi_ready, 1)
                if QT:
                    turned_query(s, par, 1)
                if Q:
                    exp_queries(s, par, 0)
                if K:
                    exp_keys(s, par, 0, None)
                if QT:
                    turned_query(s, par, 2)
                    turned_query(s, par, 3)
                if Q:
                    exp_queries(s, par, 1)
                if K:
                    exp_keys(s, par, 1, None)
                if KT:
                    turned_keys(s, par, 0)
                if QT:
                    act.wait_ge(o_part, 4 * (s - 2) + 4)
                    if not edge or s >= 4:
                        act.wait_ge(o_stored[par], 8 * (s - 2 - par))
                    act.activation(o_sb[:, par, :], acc_flat, ACT.Identity, bias=w["bias"][:, 0:1],
                                   scale=1.0).then_inc(o_copied, 1)
                if KT:
                    turned_keys(s, par, 1)
                if Q:
                    exp_queries(s, par, 2)
                if K:
                    exp_keys(s, par, 2, None)
                if KT:
                    turned_keys(s, par, 2)
                    turned_keys(s, par, 3)
                if Q:
                    exp_queries(s, par, 3)
                if K:
                    exp_keys(s, par, 3, None)
                if KT:
                    act.wait_ge(t_part, 4 * (s - 1) + 4)
                    wait_for(act, m_made, s - 1)
                    act.copy(t_hi[:, :], acc[:, 0]).then_inc(t_hi_ready, 1)
                if K:
                    act.wait_ge(shift_ready, s + 1)
                    wait_for(act, xn_lo_ready, s)
                    act.activation(xn[:, :], x_sb[:, par, :], ACT.Identity, bias=shift[:, 0:1],
                                   scale=rstd[:, 0:1]).then_inc(xn_ready, 1)
                    act.wait_ge(xn_ready, s + 1)
                    wait_for(act, q_made, 4 * (s - 1))
                    act.copy(xn_hi[:, par, :], xn[:, :]).then_inc(xn_hi_ready, 1)
                if C:
                    act.wait_ge(c_turned, s + 1)
                    wait_for(act, t_part, 4 * s)
                    act.copy(cT_hi[:, :, :].rearrange("p a b -> p (a b)"), flat("C0")).then_inc(cT_hi_ready, 1)

            each_step(act, step)

        @block.vector
        def _(dve):
            def turned_query(s, par, j):
                dve.wait_ge(q_hi_ready, 4 * (s - 2) + j + 1)
                dve.tensor_tensor(q_lo[:, j % 2, :], flat(f"QT{j}"), q_hi[:, j % 2, :].bitcast(F32),
                                  ALU.subtract).then_inc(q_lo_ready, 1)

            def turned_keys(s, par, i):
                dve.wait_ge(kT_hi_ready, 4 * (s - 1) + i + 1)
                dve.tensor_tensor(kT_lo[:, i % 2, :, :], slot(f"KT{i}"), kT_hi[:, i % 2, :, :].bitcast(F32),
                                  ALU.subtract).then_inc(kT_lo_ready, 1)

            def shift_queries(s, par, i):
                b, p = s - 1, 1 - par
                dve.wait_ge(q_made, 4 * b + i + 1)
                src = flat(f"Q{i}").rearrange("p (g d) -> p g d", d=DH)
                dve.tensor_reduce(q_max[:, i, :], src, X, ALU.max).then_inc(q_max_ready, 1)
                dve.wait_ge(q_max_ready, 4 * b + i + 1)
                dst = eq[:, p, 2 * i:2 * i + 2, :].rearrange("p n (h d) -> p (n h) d", d=DH)
                dve.tensor_tensor(dst, src, per_row(q_max[:, i, :], 2 * HEADS, DH),
                                  ALU.subtract).then_inc(q_shifted, 1)

            def sum_queries(s, par, i):
                b, p = s - 1, 1 - par
                dve.wait_ge(q_exp, 4 * b + i + 1)
                v = eq[:, p, 2 * i:2 * i + 2, :].rearrange("p n (h d) -> p (n h) d", d=DH)
                dve.tensor_reduce(q_sum[:, i, :], v, X, ALU.add).then_inc(q_summed, 1)
                dve.wait_ge(q_summed, 4 * b + i + 1)
                wait_for(dve, q_normed, 4 * b + i - 3)
                dve.reciprocal(q_inv[:, i, :], q_sum[:, i, :]).then_inc(q_inv_ready, 1)

            def min_keys(s, par, i):
                dve.wait_ge(k_made, 4 * s + i + 1)
                dve.tensor_reduce(k_min[:, par, i:i + 1], flat(f"K{i}"), X, ALU.min).then_inc(k_min_ready, 1)

            def step(s, par, edge):
                QT, M, Q, K, KT, C = (on(k, s, edge) for k in ("QT", "M", "Q", "K", "KT", "C"))
                if QT:
                    turned_query(s, par, 0)
                if M:
                    b = s - 2
                    dve.wait_ge(k_exp, 4 * b + 4)
                    dve.reciprocal(k_inv[:, :], k_sum[:, par, :]).then_inc(k_inv_ready, 1)
                    dve.wait_ge(k_inv_ready, b + 1)
                    dve.wait_ge(m_made, b + 1)
                    wait_for(dve, m_lo_ready, b)
                    made = flat("M0").rearrange("p (j h c) -> p j h c", j=CH, h=2)
                    for h in range(2):
                        r = slice(h * DH, (h + 1) * DH)
                        dve.scalar_tensor_tensor(out=m_full[r, :, :], in0=made[r, :, h, :], scalar=DH ** -0.5,
                                                 in1=per_row(k_inv[r, :], CH, P), op0=ALU.mult,
                                                 op1=ALU.mult).then_inc(m_scaled, 1)
                if Q:
                    shift_queries(s, par, 0)
                if M:
                    dve.wait_ge(m_hi_ready, s - 2 + 1)
                    dve.tensor_tensor(m_lo[:, :, :], m_full[:, :, :], m_hi[:, :, :].bitcast(F32),
                                      ALU.subtract).then_inc(m_lo_ready, 1)
                if QT:
                    turned_query(s, par, 1)
                if K:
                    min_keys(s, par, 0)
                if Q:
                    sum_queries(s, par, 0)
                if QT:
                    turned_query(s, par, 2)
                if Q:
                    shift_queries(s, par, 1)
                if QT:
                    turned_query(s, par, 3)
                if K:
                    min_keys(s, par, 1)
                if Q:
                    sum_queries(s, par, 1)
                if KT:
                    turned_keys(s, par, 0)
                if Q:
                    shift_queries(s, par, 2)
                if KT:
                    turned_keys(s, par, 1)
                if K:
                    min_keys(s, par, 2)
                    dve.wait_ge(x_loaded[par], 8 * (s - par) + 16)
                    for h in range(2):
                        dve.bn_stats(stats[:, h, :], x_sb[:, par, h * BANK:(h + 1) * BANK]).then_inc(x_stats, 1)
                    dve.drain()
                    dve.bn_aggr(mv[:, :], stats[:, :, :]).then_inc(x_mean_ready, 1)
                    dve.wait_ge(x_mean_ready, s + 1)
                    wait_for(dve, rstd_ready, s)
                    dve.tensor_scalar(veps[:, :], mv[:, 1:2], EPS, None, ALU.add).then_inc(veps_ready, 1)
                if Q:
                    sum_queries(s, par, 2)
                if KT:
                    turned_keys(s, par, 2)
                if K:
                    dve.wait_ge(rstd_ready, s + 1)
                    wait_for(dve, xn_ready, s)
                    dve.scalar_tensor_tensor(out=shift[:, :], in0=mv[:, 0:1], scalar=-1.0, in1=rstd[:, :],
                                             op0=ALU.mult, op1=ALU.mult).then_inc(shift_ready, 1)
                if Q:
                    shift_queries(s, par, 3)
                if KT:
                    turned_keys(s, par, 3)
                if K:
                    min_keys(s, par, 3)
                if Q:
                    sum_queries(s, par, 3)
                if KT:
                    dve.wait_ge(t_hi_ready, s - 1 + 1)
                    dve.tensor_tensor(t_lo[:, :], acc[:, 0], t_hi[:, :].bitcast(F32),
                                      ALU.subtract).then_inc(t_lo_ready, 1)
                if C:
                    dve.wait_ge(cT_hi_ready, s + 1)
                    dve.tensor_tensor(cT_lo[:, :, :].rearrange("p a b -> p (a b)"), flat("C0"),
                                      cT_hi[:, :, :].rearrange("p a b -> p (a b)").bitcast(F32),
                                      ALU.subtract).then_inc(cT_lo_ready, 1)

            each_step(dve, step)

        @block.tensor
        def _(pe):
            def keys(s, par, i, edge):
                wait_slot(pe, f"K{i}", s, edge)
                if i == 0:
                    pe.wait_ge(ctx_lo_ready, s + 1)
                out = slot(f"K{i}")
                for n in range(2):
                    c = slice(n * BANK, (n + 1) * BANK)
                    last = split_products(pe, out[:, n], w["k_hi"][:, i * P:(i + 1) * P], w["k_lo"][:, i * P:(i + 1) * P],
                                          ctx_hi[:, par, c], ctx_lo[:, par, c], True, True)
                last.then_inc(k_made, 1)

            def queries(s, par, i, edge):
                wait_slot(pe, f"Q{i}", s, edge)
                if i == 0:
                    pe.wait_ge(xn_lo_ready, s - 1 + 1)
                out = slot(f"Q{i}")
                for n in range(2):
                    c = slice((2 * i + n) * P, (2 * i + n + 1) * P)
                    last = split_products(pe, out[:, n], xn_hi[:, 1 - par, c], xn_lo[:, 1 - par, c],
                                          w["q_hi"][:, :], w["q_lo"][:, :], True, True)
                last.then_inc(q_made, 1)

            def turn_query(s, par, j, edge):
                wait_slot(pe, f"QT{j}", s, edge)
                pe.wait_ge(q_normed, 4 * (s - 2) + 4)
                out = flat(f"QT{j}")
                for n in range(NCH):
                    last = pe.transpose(out[:, n * P:(n + 1) * P], eq[:, par, n, j * P:(j + 1) * P], ident[:, :])
                last.then_inc(q_turned, 1)

            def turn_keys(s, par, i, edge):
                wait_slot(pe, f"KT{i}", s, edge)
                pe.wait_ge(k_exp, 4 * (s - 1) + 4)
                out = slot(f"KT{i}")
                for n in range(2):
                    for j in range(CH):
                        c = (2 * i + n) * P
                        last = pe.transpose(out[:, n, j * P:(j + 1) * P], ek[:, 1 - par, j, c:c + P], ident[:, :])
                last.then_inc(kT_turned, 1)

            def turn_context(s, par, edge):
                wait_slot(pe, "C0", s, edge)
                pe.wait_ge(ctx_loaded[par], 8 * (s - par) + 16)
                out = flat("C0")
                for n in range(NCH):
                    last = pe.transpose(out[:, n * P:(n + 1) * P], ctx_sb[:, par, n * P:(n + 1) * P], ident[:, :])
                last.then_inc(c_turned, 1)

            def add_output(s, par, j):
                pe.wait_ge(q_lo_ready, 4 * (s - 2) + j + 1)
                if j == 0:
                    pe.wait_ge(m_lo_ready, s - 2 + 1)
                    wait_for(pe, t_lo_ready, s - 2 + 1)
                for n in range(2):
                    c = slice(n * BANK, (n + 1) * BANK)
                    last = split_products(pe, acc[:, n], m_hi[:, j, :], m_lo[:, j, :], q_hi[:, j % 2, c],
                                          q_lo[:, j % 2, c], j == 0, j == CH - 1)
                last.then_inc(o_part, 1)

            def add_weighted(s, par, i):
                b = s - 1
                pe.wait_ge(kT_lo_ready, 4 * b + i + 1)
                if i == 0:
                    pe.wait_ge(cT_lo_ready, b + 1)
                    wait_for(pe, o_copied, b)
                for n in range(2):
                    last = split_products(pe, acc[:, 0], cT_hi[:, 2 * i + n, :], cT_lo[:, 2 * i + n, :],
                                          kT_hi[:, i % 2, n, :], kT_lo[:, i % 2, n, :],
                                          i == 0 and n == 0, i == CH - 1 and n == 1)
                last.then_inc(t_part, 1)

            def fold(s, par, edge):
                wait_slot(pe, "M0", s, edge)
                pe.wait_ge(t_lo_ready, s - 2 + 1)
                for j in range(CH):
                    out = flat("M0")[:, 2 * j * P:2 * (j + 1) * P]
                    c, z = slice(j * P, (j + 1) * P), slice(2 * j * P, 2 * (j + 1) * P)
                    last = split_products(pe, out, t_hi[:, c], t_lo[:, c], w["z_hi"][:, z], w["z_lo"][:, z], True, True)
                last.then_inc(m_made, 1)

            def step(s, par, edge):
                QT, M, Q, K, KT, C = (on(k, s, edge) for k in ("QT", "M", "Q", "K", "KT", "C"))
                if QT:
                    turn_query(s, par, 0, edge)
                if M:
                    fold(s, par, edge)
                if Q:
                    queries(s, par, 0, edge)
                if QT:
                    turn_query(s, par, 1, edge)
                if K:
                    keys(s, par, 0, edge)
                if QT:
                    add_output(s, par, 0)
                    turn_query(s, par, 2, edge)
                if Q:
                    queries(s, par, 1, edge)
                if QT:
                    add_output(s, par, 1)
                    turn_query(s, par, 3, edge)
                if K:
                    keys(s, par, 1, edge)
                if QT:
                    add_output(s, par, 2)
                if KT:
                    turn_keys(s, par, 0, edge)
                if Q:
                    queries(s, par, 2, edge)
                if QT:
                    add_output(s, par, 3)
                if KT:
                    turn_keys(s, par, 1, edge)
                if K:
                    keys(s, par, 2, edge)
                if KT:
                    add_weighted(s, par, 0)
                    turn_keys(s, par, 2, edge)
                if Q:
                    queries(s, par, 3, edge)
                if KT:
                    add_weighted(s, par, 1)
                    turn_keys(s, par, 3, edge)
                if K:
                    keys(s, par, 3, edge)
                if KT:
                    add_weighted(s, par, 2)
                    add_weighted(s, par, 3)
                if C:
                    turn_context(s, par, edge)

            each_step(pe, step)


def mix_weights(nc, ident, ps, w, A, B, Wr):
    RAW = 4
    with ExitStack() as ctx:
        def sem(name):
            return ctx.enter_context(nc.semaphore(name))

        raw = ctx.enter_context(nc.sbuf_tensor("raw", [P, RAW, N], F32))
        raw_loaded = [sem(f"raw_loaded{i}") for i in range(RAW)]
        b_rows = ctx.enter_context(nc.sbuf_tensor("b_rows", [P, 2, NCH, P], F32))
        b_ordered = sem("b_ordered")
        raw_turned, w_hi_ready, w_lo_ready = sem("raw_turned"), sem("w_hi_ready"), sem("w_lo_ready")
        a_v = A.rearrange("k r d -> (k r) d")
        JOBS = 2 * KCH + 1
        block = ctx.enter_context(nc.Block())

        def part(which, n):
            if n < KCH:
                return w[f"a_{which}"][:, :, n * P:(n + 1) * P]
            if n < 2 * KCH:
                return w[f"b_{which}"][:, n - KCH, :].rearrange("q (p j) -> q j p", j=NCH)
            return w[f"r_{which}"][:, :, :]

        def turned(n):
            width = P if n < 2 * KCH else EXPERTS
            return ps[:, n % 4].rearrange("p a (b c) -> p (a b) c", c=P)[:, :, 0:width]

        @block.sync
        def _(sp):
            for n in range(JOBS):
                if n >= RAW:
                    sp.wait_ge(raw_turned, n - RAW + 1)
                    wait_for(sp, b_ordered, n - RAW + 1 - KCH)
                dst = raw[:, n % RAW, :]
                if n < KCH:
                    src = a_v[n * P:(n + 1) * P, :]
                elif n < 2 * KCH:
                    src = B[(n - KCH) * 8:(n - KCH + 1) * 8].rearrange("k (p j) r -> p k (j r)", j=NCH)
                    dst = dst.rearrange("p (k m) -> p k m", k=8)
                else:
                    src, dst = Wr, dst[0:EXPERTS, :]
                sp.dma_start(dst, src).then_inc(raw_loaded[n % RAW], 16)

        @block.gpsimd
        def _(pool):
            for m in range(KCH):
                n = KCH + m
                pool.wait_ge(raw_loaded[n % RAW], 16 * (n // RAW + 1))
                if m >= 2:
                    pool.wait_ge(raw_turned, n - 2 + 1)
                pool.tensor_scalar(b_rows[:, m % 2, :, :].rearrange("p j (k r) -> p k j r", k=8),
                                   raw[:, n % RAW, :].rearrange("p (k j r) -> p k j r", k=8, j=NCH), 1.0, None,
                                   ALU.mult).then_inc(b_ordered, 1)

        @block.tensor
        def _(pe):
            for n in range(JOBS):
                if KCH <= n < 2 * KCH:
                    pe.wait_ge(b_ordered, n - KCH + 1)
                else:
                    pe.wait_ge(raw_loaded[n % RAW], 16 * (n // RAW + 1))
                if n >= 4:
                    pe.wait_ge(w_lo_ready, n - 4 + 1)
                for m in range(NCH):
                    if n < KCH:
                        src = raw[:, n % RAW, m * P:(m + 1) * P]
                    elif n < 2 * KCH:
                        src = b_rows[:, n % 2, m, :]
                    else:
                        src = raw[0:EXPERTS, n % RAW, m * P:(m + 1) * P]
                    k = src.shape[0]
                    last = pe.transpose(turned(n)[:, m, :], src, ident[0:k, 0:k])
                last.then_inc(raw_turned, 1)

        @block.scalar
        def _(act):
            for n in range(JOBS):
                act.wait_ge(raw_turned, n + 1)
                act.copy(part("hi", n), turned(n)).then_inc(w_hi_ready, 1)

        @block.vector
        def _(dve):
            for n in range(JOBS):
                dve.wait_ge(w_hi_ready, n + 1)
                dve.tensor_tensor(part("lo", n), turned(n), part("hi", n).bitcast(F32),
                                  ALU.subtract).then_inc(w_lo_ready, 1)


def expert_mix(nc, ident, ps, w, x, o_dram, out):
    with ExitStack() as ctx:
        def sb(name, shape, dt=F32):
            return ctx.enter_context(nc.sbuf_tensor(name, shape, dt))

        def sem(name):
            return ctx.enter_context(nc.semaphore(name))

        x_sb = sb("x2_in", [P, 2, N])
        o_sb = sb("o_in", [P, 2, N])
        x2 = sb("x2", [P, 2, N])
        sq = sb("sq", [P, N])
        y = sb("y", [P, N])
        xn = sb("xn2", [P, N])
        xT_hi = sb("xT_hi", [P, NCH, P], F32R)
        xT_lo = sb("xT_lo", [P, NCH, P], F32R)
        hg = sb("hg", [P, KR])
        hT_hi = sb("hT_hi", [P, KCH, P], F32R)
        hT_lo = sb("hT_lo", [P, KCH, P], F32R)
        var_c = sb("var_c", [P, NCH])
        rstd_c = sb("rstd_c", [P, NCH])
        stats = sb("stats2", [P, 2, 6])
        mv = sb("mv2", [P, 2])
        veps = sb("veps2", [P, 1])
        rstd = sb("rstd2", [P, 1])
        shift = sb("shift2", [P, 1])
        score = sb("score", [P, EXPERTS])
        top = sb("top", [P, 2, 8])
        neg_top = sb("neg_top", [P, 1])
        rest = sb("rest", [P, 2, EXPERTS])
        e_all = sb("e_all", [P, EXPERTS])
        e_rest = sb("e_rest", [P, EXPERTS])
        gate_sum = sb("gate_sum", [P, 1])
        gate_inv = sb("gate_inv", [P, 1])
        gate_raw = sb("gate_raw", [P, EXPERTS])
        gate = sb("gate", [P, EXPERTS])

        x_loaded = [sem(f"x2_loaded{i}") for i in range(2)]
        o_loaded = [sem(f"o_loaded{i}") for i in range(2)]
        stored = [sem(f"stored{i}") for i in range(2)]
        o_turned, y_turned, x_turned, scored = sem("o_turned"), sem("y_turned"), sem("x_turned"), sem("scored")
        h_made, h_turned, r_made = sem("h_made"), sem("h_turned"), sem("r_made")
        squared, xn_ready, x_hi_ready, h_hi_ready = sem("squared"), sem("xn2_ready"), sem("x_hi_ready"), sem("h_hi_ready")
        scores_copied, e_all_ready, e_rest_ready = sem("scores_copied"), sem("e_all_ready"), sem("e_rest_ready")
        var_sum, var_ready, y_ready, x2_ready = sem("var_sum"), sem("var_ready"), sem("y_ready"), sem("x2_ready")
        x2_stats, x2_mean, veps_ready, shift_ready = sem("x2_stats"), sem("x2_mean"), sem("veps2_ready"), sem("shift_ready")
        rstd_c_ready, rstd_ready = sem("rstd_c_ready"), sem("rstd2_ready")
        x_lo_ready, h_lo_ready, h_gated, added = sem("x_lo_ready"), sem("h_lo_ready"), sem("h_gated"), sem("added")
        top_step, neg_top_ready, gate_step, gates_ready = sem("top_step"), sem("neg_top_ready"), sem("gate_step"), sem("gates_ready")

        ring = [ps[:, 0], ps[:, 1]]
        OT, YT, XT, SC = ring[0], ring[1], ring[1], ring[1][:, 0, 0:EXPERTS]
        HT = ring[0][:, 0]
        H, R = ps[:, 2], ps[:, 3]
        flat = "p a b -> p (a b)"

        def each_step(eng, step):
            for t in (-1, 0, 1, 2):
                step(t, t % 2, t >= 0, True)
            with eng.Fori(0, (BATCHES - 4) // 2) as i:
                for k in range(2):
                    step(2 * i + 3 + k, (3 + k) % 2, True, True)
            step(BATCHES - 1, (BATCHES - 1) % 2, True, False)

        block = ctx.enter_context(nc.Block())

        @block.sync
        def _(sp):
            def load(b, p):
                wait_for(sp, o_turned, b - 1)
                sp.dma_start(o_sb[:, p, :], o_dram[b]).then_inc(o_loaded[p], 16)
                wait_for(sp, x2_ready, b - 1)
                sp.dma_start(x_sb[:, p, :], x[b]).then_inc(x_loaded[p], 16)

            def step(t, par, mix, ahead):
                if ahead and (not isinstance(t, int) or t + 2 < BATCHES):
                    load_ok = True
                    load(t + 2, par)
                if mix:
                    sp.wait_ge(added, t + 1)
                    sp.dma_start(out[t], x2[:, par, :]).then_inc(stored[par], 16)

            load(0, 0)
            for t in (-1, 0, 1, 2):
                step(t, t % 2, t >= 0, True)
            with sp.Fori(0, (BATCHES - 4) // 2 - 1) as i:
                for k in range(2):
                    step(2 * i + 3 + k, (3 + k) % 2, True, True)
            for t in range(BATCHES - 3, BATCHES):
                step(t, t % 2, True, True)
            for sem_ in stored:
                sp.wait_ge(sem_, 16 * BATCHES // 2)

        @block.gpsimd
        def _(pool):
            def step(t, par, mix, ahead):
                if ahead:
                    b = t + 1
                    pool.wait_ge(var_ready, b + 1)
                    wait_for(pool, y_ready, b)
                    pool.tensor_tensor(rstd_c[:, :], var_c[:, :], w["minus_half"][:, 0:1].broadcast_to([P, NCH]),
                                       ALU.pow).then_inc(rstd_c_ready, 1)
                    pool.wait_ge(veps_ready, b + 1)
                    wait_for(pool, xn_ready, b)
                    pool.tensor_tensor(rstd[:, :], veps[:, :], w["minus_half"][:, :], ALU.pow).then_inc(rstd_ready, 1)

            each_step(pool, step)

        @block.scalar
        def _(act):
            def turned_hidden(t, half):
                act.wait_ge(h_turned, 2 * t + half + 1)
                if half == 0:
                    wait_for(act, r_made, t)
                dst = hT_hi[:, half * 4:half * 4 + 4, :].rearrange(flat)
                act.copy(dst, HT).then_inc(h_hi_ready, 1)

            def step(t, par, mix, ahead):
                b = t + 1
                if ahead:
                    act.wait_ge(o_turned, b + 1)
                    wait_for(act, var_sum, b)
                    act.activation(sq[:, :], OT.rearrange(flat), ACT.Square).then_inc(squared, 1)
                if mix:
                    turned_hidden(t, 0)
                if ahead:
                    act.wait_ge(shift_ready, b + 1)
                    wait_for(act, x_turned, b)
                    act.activation(xn[:, :], x2[:, 1 - par, :], ACT.Identity, bias=shift[:, 0:1],
                                   scale=rstd[:, 0:1]).then_inc(xn_ready, 1)
                    act.wait_ge(x_turned, b + 1)
                    wait_for(act, h_made, 2 * b)
                    act.copy(xT_hi[:, :, :].rearrange(flat), XT.rearrange(flat)).then_inc(x_hi_ready, 1)
                if mix:
                    turned_hidden(t, 1)
                if ahead:
                    act.wait_ge(neg_top_ready, b + 1)
                    wait_for(act, gate_step, 3 * b)
                    act.activation(e_all[:, :], score[:, :], ACT.Exp, bias=neg_top[:, 0:1],
                                   scale=1.0).then_inc(e_all_ready, 1)
                    act.wait_ge(top_step, 2 * b + 2)
                    act.activation(e_rest[:, :], rest[:, 1, :], ACT.Exp, bias=neg_top[:, 0:1],
                                   scale=1.0).then_inc(e_rest_ready, 1)

            each_step(act, step)

        @block.vector
        def _(dve):
            def gate_hidden(t, half):
                dve.wait_ge(h_made, 2 * t + half + 1)
                if half == 0:
                    dve.wait_ge(gates_ready, t + 1)
                wait_for(dve, h_turned, 2 * (t - 1) + half + 1)
                g0 = half * EXPERTS // 2
                v = hg[:, half * BANK:(half + 1) * BANK].rearrange("p (k r) -> p k r", r=RANK)
                dve.tensor_tensor(v, H[:, half].rearrange("p (k r) -> p k r", r=RANK),
                                  per_row(gate[:, g0:g0 + EXPERTS // 2], EXPERTS // 2, RANK),
                                  ALU.mult).then_inc(h_gated, 1)

            def turned_hidden(t, half):
                dve.wait_ge(h_hi_ready, 2 * t + half + 1)
                c = slice(half * 4, half * 4 + 4)
                dve.tensor_tensor(hT_lo[:, c, :].rearrange(flat), HT, hT_hi[:, c, :].rearrange(flat).bitcast(F32),
                                  ALU.subtract).then_inc(h_lo_ready, 1)

            def gates(b):
                dve.wait_ge(scored, b + 1)
                wait_for(dve, e_all_ready, b)
                dve.tensor_copy(score[:, :], SC).then_inc(scores_copied, 1)
                dve.drain()
                dve.max(top[:, 0, :], score[:, :]).then_inc(top_step, 1)
                dve.wait_ge(top_step, 2 * b + 1)
                wait_for(dve, e_rest_ready, b)
                dve.tensor_scalar(neg_top[:, :], top[:, 0, 0:1], -1.0, None, ALU.mult).then_inc(neg_top_ready, 1)
                dve.match_replace(rest[:, 0, :], top[:, 0, :], score[:, :], LOWEST)
                dve.drain()
                dve.max(top[:, 1, :], rest[:, 0, :])
                dve.drain()
                dve.match_replace(rest[:, 1, :], top[:, 1, :], rest[:, 0, :], LOWEST).then_inc(top_step, 1)
                dve.wait_ge(e_all_ready, b + 1)
                dve.wait_ge(e_rest_ready, b + 1)
                dve.tensor_tensor(gate_raw[:, :], e_all[:, :], e_rest[:, :], ALU.subtract).then_inc(gate_step, 1)
                dve.wait_ge(gate_step, 3 * b + 1)
                dve.tensor_reduce(gate_sum[:, :], gate_raw[:, :], X, ALU.add).then_inc(gate_step, 1)
                dve.wait_ge(gate_step, 3 * b + 2)
                dve.reciprocal(gate_inv[:, :], gate_sum[:, :]).then_inc(gate_step, 1)
                dve.wait_ge(gate_step, 3 * b + 3)
                dve.tensor_scalar(gate[:, :], gate_raw[:, :], gate_inv[:, 0:1], MIX_SCALE, ALU.mult,
                                  ALU.mult).then_inc(gates_ready, 1)

            def step(t, par, mix, ahead):
                b, p = t + 1, 1 - par
                if ahead:
                    dve.wait_ge(squared, b + 1)
                    dve.tensor_reduce(var_c[:, :], sq[:, :].rearrange("p (n c) -> p n c", c=P), X,
                                      ALU.add).then_inc(var_sum, 1)
                    dve.wait_ge(var_sum, b + 1)
                    dve.tensor_scalar(var_c[:, :], var_c[:, :], 1.0 / P, EPS, ALU.mult, ALU.add).then_inc(var_ready, 1)
                    dve.wait_ge(rstd_c_ready, b + 1)
                    wait_for(dve, y_turned, b)
                    dve.tensor_tensor(y[:, :].rearrange("p (n c) -> p n c", c=P),
                                      OT.rearrange("p a (b c) -> p (a b) c", c=P), per_row(rstd_c[:, :], NCH, P),
                                      ALU.mult).then_inc(y_ready, 1)
                if mix:
                    gate_hidden(t, 0)
                if ahead:
                    dve.wait_ge(y_turned, b + 1)
                    dve.wait_ge(x_loaded[p], 8 * (b - p) + 16)
                    if not isinstance(t, int) or b >= 2:
                        dve.wait_ge(stored[p], 8 * (b - p))
                    dve.scalar_tensor_tensor(out=x2[:, p, :], in0=YT.rearrange(flat), scalar=w["g"][:, 0:1],
                                             in1=x_sb[:, p, :], op0=ALU.mult, op1=ALU.add).then_inc(x2_ready, 1)
                    dve.wait_ge(x2_ready, b + 1)
                    for h in range(2):
                        dve.bn_stats(stats[:, h, :], x2[:, p, h * BANK:(h + 1) * BANK]).then_inc(x2_stats, 1)
                    dve.drain()
                    dve.bn_aggr(mv[:, :], stats[:, :, :]).then_inc(x2_mean, 1)
                    dve.wait_ge(x2_mean, b + 1)
                    dve.tensor_scalar(veps[:, :], mv[:, 1:2], EPS, None, ALU.add).then_inc(veps_ready, 1)
                    dve.wait_ge(rstd_ready, b + 1)
                    dve.scalar_tensor_tensor(out=shift[:, :], in0=mv[:, 0:1], scalar=-1.0, in1=rstd[:, :],
                                             op0=ALU.mult, op1=ALU.mult).then_inc(shift_ready, 1)
                if mix:
                    turned_hidden(t, 0)
                    gate_hidden(t, 1)
                if ahead:
                    dve.wait_ge(x_hi_ready, b + 1)
                    dve.tensor_tensor(xT_lo[:, :, :].rearrange(flat), XT.rearrange(flat),
                                      xT_hi[:, :, :].rearrange(flat).bitcast(F32), ALU.subtract).then_inc(x_lo_ready, 1)
                if mix:
                    turned_hidden(t, 1)
                if ahead:
                    gates(b)
                if mix:
                    dve.wait_ge(r_made, t + 1)
                    dve.tensor_tensor(x2[:, par, :], R.rearrange(flat), x2[:, par, :], ALU.add).then_inc(added, 1)

            each_step(dve, step)

        @block.tensor
        def _(pe):
            def turn(dst, src, done):
                for n in range(src.shape[1] // P):
                    last = pe.transpose(dst[:, n * P:(n + 1) * P], src[:, n * P:(n + 1) * P], ident[:, :])
                last.then_inc(done, 1)

            def hidden(half, chunks):
                for n in chunks:
                    last = split_products(pe, H[:, half], xT_hi[:, n, :], xT_lo[:, n, :],
                                          w["a_hi"][:, n, half * BANK:(half + 1) * BANK],
                                          w["a_lo"][:, n, half * BANK:(half + 1) * BANK], n == 0, n == NCH - 1)
                return last

            def result(chunks):
                for q in chunks:
                    for d in range(2):
                        last = split_products(pe, R[:, d], hT_hi[:, q, :], hT_lo[:, q, :],
                                              w["b_hi"][:, q, d * BANK:(d + 1) * BANK],
                                              w["b_lo"][:, q, d * BANK:(d + 1) * BANK], q == 0, q == KCH - 1)
                return last

            def step(t, par, mix, ahead):
                b, p = t + 1, 1 - par
                if ahead:
                    pe.wait_ge(o_loaded[p], 8 * (b - p) + 16)
                    wait_for(pe, h_lo_ready, 2 * t)
                    turn(OT.rearrange(flat), o_sb[:, p, :], o_turned)
                if mix:
                    pe.wait_ge(x_lo_ready, t + 1)
                    wait_for(pe, h_gated, 2 * t)
                    hidden(0, range(NCH)).then_inc(h_made, 1)
                if ahead:
                    pe.wait_ge(y_ready, b + 1)
                    wait_for(pe, scores_copied, b)
                    turn(YT.rearrange(flat), y[:, :], y_turned)
                if mix:
                    hidden(1, range(NCH // 2))
                    pe.wait_ge(h_gated, 2 * t + 1)
                    if not ahead:
                        pe.wait_ge(h_lo_ready, 2 * t)
                    turn(HT, hg[:, 0:BANK], h_turned)
                    hidden(1, range(NCH // 2, NCH)).then_inc(h_made, 1)
                if ahead:
                    pe.wait_ge(xn_ready, b + 1)
                    pe.wait_ge(x2_ready, b + 1)
                    turn(XT.rearrange(flat), xn[:, :], x_turned)
                if mix:
                    pe.wait_ge(h_lo_ready, 2 * t + 1)
                    wait_for(pe, added, t)
                    result(range(1))
                    pe.wait_ge(h_gated, 2 * t + 2)
                    turn(HT, hg[:, BANK:2 * BANK], h_turned)
                    result(range(1, KCH // 2))
                if ahead:
                    pe.wait_ge(x_lo_ready, b + 1)
                    for n in range(NCH):
                        last = split_products(pe, SC, xT_hi[:, n, :], xT_lo[:, n, :], w["r_hi"][:, n, :],
                                              w["r_lo"][:, n, :], n == 0, n == NCH - 1)
                    last.then_inc(scored, 1)
                if mix:
                    pe.wait_ge(h_lo_ready, 2 * t + 2)
                    result(range(KCH // 2, KCH)).then_inc(r_made, 1)

            each_step(pe, step)


def xattn_ffn(nc, x, context, Wq, Wkv, Wout, b_out, g, A, B, Wr, out):
    o_dram = nc.dram_tensor("attention_out", (BATCHES, P, N), F32).ap()
    with ExitStack() as ctx:
        def sb(name, shape, dt=F32):
            return ctx.enter_context(nc.sbuf_tensor(name, shape, dt))

        ps = ctx.enter_context(nc.psum_tensor("ps", [P, 4, 2, BANK], F32))
        ident = sb("ident", [P, P])
        w = {"g": sb("g_col", [P, 1]), "bias": sb("bias_col", [P, 1]), "minus_half": sb("minus_half", [P, 1]),
             "one": sb("one", [P, 1])}
        with ExitStack() as first:
            for name, width in (("q", HD), ("k", HD), ("z", 2 * HD)):
                for part in ("hi", "lo"):
                    w[f"{name}_{part}"] = first.enter_context(nc.sbuf_tensor(f"w_{name}_{part}", [P, width], F32R))
            attention_weights(nc, ident, ps, w, Wq, Wkv, Wout, b_out, g)
            attention(nc, ident, ps, w, x, context, o_dram)
        for part in ("hi", "lo"):
            w[f"a_{part}"] = sb(f"w_a_{part}", [P, NCH, KR], F32R)
            w[f"b_{part}"] = sb(f"w_b_{part}", [P, KCH, N], F32R)
            w[f"r_{part}"] = sb(f"w_r_{part}", [P, NCH, EXPERTS], F32R)
        mix_weights(nc, ident, ps, w, A, B, Wr)
        expert_mix(nc, ident, ps, w, x, o_dram, out)


_INS = ["x", "ctx_4096", "L0_xattn_Wq", "L0_xattn_Wkv", "L0_xattn_Wout", "L0_xattn_b_out", "L0_xattn_g",
        "L0_ffn_A", "L0_ffn_B", "L0_ffn_Wr"]


def kernel(**inputs):
    import numpy as _np
    import concourse.bacc as _bacc
    from concourse import mybir as _mybir
    from concourse.bass_utils import run_bass_kernel_spmd as _run

    nc = _bacc.Bacc("TRN2", target_bir_lowering=False, num_devices=1)
    arrays, args = {}, []
    for name in _INS:
        a = _np.ascontiguousarray(inputs[name])
        arrays[f"in_{name}"] = a
        args.append(nc.dram_tensor(f"in_{name}", a.shape, _mybir.dt.from_np(a.dtype), kind="ExternalInput").ap())
    args.append(nc.dram_tensor("out_0", (BATCHES, P, N), F32, kind="ExternalOutput").ap())
    xattn_ffn(nc, *args)
    r = _run(nc, [arrays], core_ids=[0])
    return r.results[0]["out_0"]
```

```python
from contextlib import ExitStack

import concourse.bass as bass
from concourse import mybir

F32 = mybir.dt.float32
F32R = mybir.dt.float32r
ALU = mybir.AluOpType
ACT = mybir.ActivationFunctionType
X = mybir.AxisListType.X

P = 128
BANK = 512
BATCHES, N = 32, 1024
HEADS, DH = 8, 64
HD = HEADS * DH
CH = HD // P
NCH = N // P
EXPERTS, RANK, TOPK = 64, 16, 16
KR = EXPERTS * RANK
KCH = KR // P
EPS = 1e-5
MIX_SCALE = 32.0 / RANK
LOWEST = -3.4028234e38


def wait_for(eng, sem, value):
    if isinstance(value, int) and value <= 0:
        return
    eng.wait_ge(sem, value)


def per_row(col, groups, width):
    return col.unsqueeze(2).broadcast_to([col.shape[0], groups, width])


def split_products(pe, out, stat_hi, stat_lo, mov_hi, mov_lo, first, last):
    pe.matmul(out, stat_hi, mov_hi, start=first, stop=False)
    pe.matmul(out, stat_hi, mov_lo, start=False, stop=False)
    return pe.matmul(out, stat_lo, mov_hi, start=False, stop=last)


def attention_weights(nc, ident, ps, w, Wq, Wkv, Wout, b_out, g):
    with ExitStack() as ctx:
        def sb(name, shape, dt=F32):
            return ctx.enter_context(nc.sbuf_tensor(name, shape, dt))

        def sem(name):
            return ctx.enter_context(nc.semaphore(name))

        wq_raw = sb("wq_raw", [P, CH, P])
        wk_raw = sb("wk_raw", [P, CH, P])
        wv_raw = sb("wv_raw", [P, CH, P])
        wo_raw = sb("wo_raw", [P, HD])
        b_rows = sb("bias_rows", [P, P])
        b_col = sb("b_col", [P, 1])
        b_mean = sb("b_mean", [P, 1])
        wo_sum = sb("wo_sum", [P, CH])
        wo_mean = sb("wo_mean", [P, CH])
        wo_pairs = sb("wo_pairs", [P, CH, 2, P])

        weights_loaded = sem("weights_loaded")
        ident_zeroed = sem("ident_zeroed")
        ident_ready = sem("ident_ready")
        turned = sem("turned")
        wo_step = sem("wo_step")
        b_step = sem("b_step")
        wo_centred = sem("wo_centred")
        hi_ready = sem("hi_ready")
        lo_ready = sem("lo_ready")
        folded = sem("folded")
        qT, kT, oT, z = ps[:, 0, 0], ps[:, 0, 1], ps[:, 1, 0], ps[:, 2]
        block = ctx.enter_context(nc.Block())

        @block.sync
        def _(sp):
            for dst, src in ((wq_raw[:, :, :], Wq.rearrange("(j p) c -> p j c", p=P)),
                             (wk_raw[:, :, :], Wkv[0:HD, :].rearrange("(j p) c -> p j c", p=P)),
                             (wv_raw[:, :, :], Wkv[HD:2 * HD, :].rearrange("(j p) c -> p j c", p=P)),
                             (wo_raw[:, :], Wout),
                             (b_rows[:, :], b_out.rearrange("(a c) -> a c", a=1).broadcast_to([P, P])),
                             (b_col[:, :], b_out.rearrange("(c a) -> c a", a=1)),
                             (w["g"][:, :], g.rearrange("a c b -> (a c) b"))):
                sp.dma_start(dst, src).then_inc(weights_loaded, 16)

        @block.gpsimd
        def _(pool):
            pool.memset(w["minus_half"][:, :], -0.5)
            pool.memset(w["one"][:, :], 1.0)
            pool.memset(ident[:, :], 0.0).then_inc(ident_zeroed, 1)
            pool.wait_ge(ident_zeroed, 1)
            pool.affine_select(out=ident[:, :], in_=ident[:, :], compare_op=ALU.not_equal, fill=1.0,
                               base=0, pattern=[[-1, P]], channel_multiplier=1).then_inc(ident_ready, 1)

        @block.tensor
        def _(pe):
            pe.wait_ge(weights_loaded, 7 * 16)
            pe.wait_ge(ident_ready, 1)
            for j in range(CH):
                pe.transpose(qT[:, j * P:(j + 1) * P], wq_raw[:, j, :], ident[:, :])
            for j in range(CH):
                pe.transpose(kT[:, j * P:(j + 1) * P], wk_raw[:, j, :], ident[:, :])
            for j in range(CH):
                last = pe.transpose(oT[:, j * P:(j + 1) * P], wo_raw[:, j * P:(j + 1) * P], ident[:, :])
            last.then_inc(turned, 1)
            pe.wait_ge(wo_centred, 2)
            for j in range(CH):
                last = pe.matmul(z[:, j // 2, (j % 2) * 2 * P:(j % 2 + 1) * 2 * P], wv_raw[:, j, :],
                                 wo_pairs[:, j, :, :], start=True, stop=True)
            last.then_inc(folded, 1)

        @block.vector
        def _(dve):
            dve.memset(wo_pairs[:, :, :, :], 0.0).then_inc(wo_step, 1)
            dve.wait_ge(weights_loaded, 7 * 16)
            dve.reduce_sum(b_mean[:, :], b_rows[:, :], axis=X).then_inc(b_step, 1)
            dve.wait_ge(b_step, 1)
            dve.tensor_scalar(b_mean[:, :], b_mean[:, :], 1.0 / P, None, ALU.mult).then_inc(b_step, 1)
            dve.wait_ge(b_step, 2)
            dve.tensor_tensor(w["bias"][:, :], b_col[:, :], b_mean[:, :], ALU.subtract)
            dve.wait_ge(turned, 1)
            oT3 = oT.rearrange("p (j c) -> p j c", j=CH)
            dve.reduce_sum(wo_sum[:, :], oT3, axis=X).then_inc(wo_step, 1)
            dve.wait_ge(wo_step, 2)
            dve.tensor_scalar(wo_mean[:, :], wo_sum[:, :], 1.0 / P, None, ALU.mult).then_inc(wo_step, 1)
            dve.wait_ge(wo_step, 3)
            for h in range(2):
                r = slice(h * DH, (h + 1) * DH)
                dve.tensor_tensor(wo_pairs[r, :, h, :], oT3[r, :, :], per_row(wo_mean[r, :], CH, P),
                                  ALU.subtract).then_inc(wo_centred, 1)
            dve.tensor_copy(w["q_hi"][:, :], qT).then_inc(hi_ready, 1)
            dve.tensor_scalar(w["k_hi"][:, :], kT, -1.0, None, ALU.mult).then_inc(hi_ready, 1)
            dve.wait_ge(hi_ready, 2)
            dve.tensor_tensor(w["q_lo"][:, :], qT, w["q_hi"][:, :].bitcast(F32), ALU.subtract)
            dve.scalar_tensor_tensor(out=w["k_lo"][:, :], in0=kT, scalar=-1.0, in1=w["k_hi"][:, :].bitcast(F32),
                                     op0=ALU.mult, op1=ALU.subtract)
            dve.wait_ge(folded, 1)
            z2 = ps[:, 2].rearrange("p a b -> p (a b)")
            dve.tensor_copy(w["z_hi"][:, :], z2).then_inc(hi_ready, 1)
            dve.wait_ge(hi_ready, 3)
            dve.tensor_tensor(w["z_lo"][:, :], z2, w["z_hi"][:, :].bitcast(F32), ALU.subtract)


RING = ["KT0", "Q0", "KT1", "K0", "KT2", "Q1", "KT3", "K1", "Q2",
        "QT0", "K2", "M0", "QT1", "Q3", "QT2", "K3", "QT3", "C0"]
SLOTS = 3
DELAY = {"X": -1, "K": 0, "C": 0, "Q": 0, "KT": 1, "M": 1, "QT": 1, "O": 2}
PER_BATCH = {"K": 4, "C": 1, "Q": 4, "KT": 4, "M": 1, "QT": 4}
FIRST_STEP, FULL_FROM, FULL_TO, STEPS = -1, 4, BATCHES - 2, BATCHES + 2


def attention(nc, ident, ps, w, x, context, o_dram):
    with ExitStack() as ctx:
        def sb(name, shape, dt=F32):
            return ctx.enter_context(nc.sbuf_tensor(name, shape, dt))

        def sem(name):
            return ctx.enter_context(nc.semaphore(name))

        x_sb = sb("x_sb", [P, 2, N])
        ctx_sb = sb("ctx_sb", [P, 2, N])
        ctx_hi = sb("ctx_hi", [P, 2, N], F32R)
        ctx_lo = sb("ctx_lo", [P, 2, N], F32R)
        xn = sb("xn", [P, N])
        xn_hi = sb("xn_hi", [P, 2, N], F32R)
        xn_lo = sb("xn_lo", [P, 2, N], F32R)
        cT_hi = sb("cT_hi", [P, NCH, P], F32R)
        cT_lo = sb("cT_lo", [P, NCH, P], F32R)
        ek = sb("ek", [P, 2, CH, N])
        eq = sb("eq", [P, 2, NCH, HD])
        kT = sb("kT", [P, 2, 2, HD])
        kT_hi = sb("kT_hi", [P, 2, 2, HD], F32R)
        kT_lo = sb("kT_lo", [P, 2, 2, HD], F32R)
        q_hi = sb("qh", [P, 2, N], F32R)
        q_lo = sb("ql", [P, 2, N], F32R)
        t_hi = sb("t_hi", [P, HD], F32R)
        t_lo = sb("t_lo", [P, HD], F32R)
        m_full = sb("m_full", [P, CH, P])
        m_hi = sb("m_hi", [P, CH, P], F32R)
        m_lo = sb("m_lo", [P, CH, P], F32R)
        o_sb = sb("o_sb", [P, 2, N])
        k_min = sb("k_min", [P, 2, CH])
        k_sum = sb("k_sum", [P, 2, CH])
        k_inv = sb("k_inv", [P, CH])
        q_max = sb("q_max", [P, 4, 2 * HEADS])
        q_sum = sb("q_sum", [P, 4, 2 * HEADS])
        q_inv = sb("q_inv", [P, 4, 2 * HEADS])
        stats = sb("stats", [P, 2, 6])
        mv = sb("mv", [P, 2])
        veps = sb("veps", [P, 1])
        rstd = sb("rstd", [P, 1])
        shift = sb("shift", [P, 1])

        ctx_loaded = [sem(f"ctx_loaded{i}") for i in range(2)]
        x_loaded = [sem(f"x_loaded{i}") for i in range(2)]
        o_stored = [sem(f"o_stored{i}") for i in range(2)]
        k_made, c_turned, q_made = sem("k_made"), sem("c_turned"), sem("q_made")
        kT_turned, q_turned = sem("kT_turned"), sem("q_turned")
        t_part, m_made, o_part = sem("t_part"), sem("m_made"), sem("o_part")
        k_min_ready, q_max_ready, q_shifted = sem("k_min_ready"), sem("q_max_ready"), sem("q_shifted")
        q_summed, q_inv_ready = sem("q_summed"), sem("q_inv_ready")
        q_lo_ready, cT_lo_ready = sem("q_lo_ready"), sem("cT_lo_ready")
        t_lo_ready, k_inv_ready, m_scaled, m_lo_ready = (
            sem("t_lo_ready"), sem("k_inv_ready"), sem("m_scaled"), sem("m_lo_ready"))
        x_stats, x_mean_ready, veps_ready, shift_ready = (
            sem("x_stats"), sem("x_mean_ready"), sem("veps_ready"), sem("shift_ready"))
        k_exp, q_exp, q_hi_ready = sem("k_exp"), sem("q_exp"), sem("q_hi_ready")
        kT_copied, kT_hi_ready = sem("kT_copied"), sem("kT_hi_ready")
        cT_hi_ready, t_hi_ready, m_hi_ready, o_copied = (
            sem("cT_hi_ready"), sem("t_hi_ready"), sem("m_hi_ready"), sem("o_copied"))
        xn_ready, xn_hi_ready = sem("xn_ready"), sem("xn_hi_ready")
        kT_lo_ready, q_normed = sem("kT_lo_ready"), sem("q_normed")
        ctx_hi_ready, ctx_lo_ready = sem("ctx_hi_ready"), sem("ctx_lo_ready")
        rstd_ready, xn_lo_ready = sem("rstd_ready"), sem("xn_lo_ready")

        slot_read = {"K": k_exp, "C": cT_lo_ready, "Q": q_shifted, "KT": kT_copied, "M": m_scaled,
                     "QT": q_lo_ready}

        def slot(job):
            return ps[:, RING.index(job) % SLOTS]

        def flat(job):
            return slot(job).rearrange("p a b -> p (a b)")

        acc = ps[:, SLOTS]
        acc_flat = acc.rearrange("p a b -> p (a b)")

        def on(kind, s, edge):
            return not edge or 0 <= s - DELAY[kind] < BATCHES

        def wait_slot(eng, job, s, edge):
            n, back = RING.index(job), 0
            while True:
                n -= SLOTS
                if n < 0:
                    n, back = n + len(RING), back + 1
                kind, i = RING[n][:-1], int(RING[n][-1])
                if edge and s - back < 0:
                    return
                if on(kind, s - back, edge):
                    b = s - back - DELAY[kind]
                    wait_for(eng, slot_read[kind], 2 * b + 2 if kind == "M" else PER_BATCH[kind] * b + i + 1)
                    return

        def each_step(eng, step):
            for s in range(FIRST_STEP, FULL_FROM):
                step(s, s % 2, True)
            with eng.Fori(FULL_FROM // 2, FULL_TO // 2) as i:
                for parity in range(2):
                    step(2 * i + parity, parity, False)
            for s in range(FULL_TO, STEPS):
                step(s, s % 2, True)

        STAGES = ("X", "K", "Q", "C", "KT", "M", "QT", "O")
        block = ctx.enter_context(nc.Block())

        @block.sync
        def _(sp):
            def load_context(b, p):
                wait_for(sp, ctx_lo_ready, b - 1)
                wait_for(sp, c_turned, b - 1)
                sp.dma_start(ctx_sb[:, p, :], context[b]).then_inc(ctx_loaded[p], 16)

            def load_x(b, p):
                wait_for(sp, xn_ready, b - 1)
                sp.dma_start(x_sb[:, p, :], x[b]).then_inc(x_loaded[p], 16)

            def step(s, par, edge):
                if not edge or 0 <= s + 1 < BATCHES:
                    load_context(s + 1, 1 - par)
                if not edge or 0 <= s + 2 < BATCHES:
                    load_x(s + 2, par)
                if on("O", s, edge):
                    sp.wait_ge(o_copied, s - 2 + 1)
                    sp.dma_start(o_dram[s - 2], o_sb[:, par, :]).then_inc(o_stored[par], 16)

            load_x(0, 0)
            each_step(sp, step)
            for sem_ in o_stored:
                sp.wait_ge(sem_, 16 * BATCHES // 2)

        @block.gpsimd
        def _(pool):
            def rstd_x(b):
                pool.wait_ge(veps_ready, b + 1)
                wait_for(pool, xn_ready, b)
                pool.tensor_tensor(rstd[:, :], veps[:, :], w["minus_half"][:, :], ALU.pow).then_inc(rstd_ready, 1)

            def context_hi(b, p):
                pool.wait_ge(ctx_loaded[p], 8 * (b - p) + 16)
                wait_for(pool, k_made, CH * (b - 1))
                pool.tensor_tensor(ctx_hi[:, p, :], ctx_sb[:, p, :], w["one"][:, 0:1].broadcast_to([P, N]),
                                   ALU.mult).then_inc(ctx_hi_ready, 1)

            def context_lo(b, p):
                pool.wait_ge(ctx_hi_ready, b + 1)
                pool.tensor_tensor(ctx_lo[:, p, :], ctx_sb[:, p, :], ctx_hi[:, p, :].bitcast(F32),
                                   ALU.subtract).then_inc(ctx_lo_ready, 1)

            def x_lo(b, p):
                wait_for(pool, q_made, 4 * (b - 1))
                pool.wait_ge(xn_hi_ready, b + 1)
                pool.tensor_tensor(xn_lo[:, p, :], xn[:, :], xn_hi[:, p, :].bitcast(F32),
                                   ALU.subtract).then_inc(xn_lo_ready, 1)

            def norm_queries(b, p, i):
                pool.wait_ge(q_inv_ready, 4 * b + i + 1)
                v = eq[:, p, 2 * i:2 * i + 2, :].rearrange("p n (h d) -> p (n h) d", d=DH)
                pool.tensor_tensor(v, v, per_row(q_inv[:, i, :], 2 * HEADS, DH), ALU.mult).then_inc(q_normed, 1)

            def keys_lo(b, i):
                pool.wait_ge(kT_hi_ready, 4 * b + i + 1)
                pool.tensor_tensor(kT_lo[:, i % 2, :, :], kT[:, i % 2, :, :], kT_hi[:, i % 2, :, :].bitcast(F32),
                                   ALU.subtract).then_inc(kT_lo_ready, 1)

            def step(s, par, edge):
                X_, K, Q, C, KT, M, QT, O = (on(k, s, edge) for k in STAGES)
                if KT:
                    keys_lo(s - 1, 0)
                if KT:
                    norm_queries(s - 1, 1 - par, 3)
                if KT:
                    keys_lo(s - 1, 1)
                    keys_lo(s - 1, 2)
                    keys_lo(s - 1, 3)
                if X_:
                    rstd_x(s + 1)
                if Q:
                    norm_queries(s, par, 0)
                    norm_queries(s, par, 1)
                if X_:
                    context_hi(s + 1, 1 - par)
                    context_lo(s + 1, 1 - par)
                    x_lo(s + 1, 1 - par)
                if Q:
                    norm_queries(s, par, 2)

            each_step(pool, step)

        @block.scalar
        def _(act):
            def keys_copy(b, i):
                act.wait_ge(kT_turned, 4 * b + i + 1)
                wait_for(act, kT_lo_ready, 4 * b + i - 1)
                act.copy(kT[:, i % 2, :, :], slot(f"KT{i}")).then_inc(kT_copied, 1)

            def keys_hi(b, i):
                act.wait_ge(kT_copied, 4 * b + i + 1)
                wait_for(act, t_part, 4 * b + i - 1)
                act.copy(kT_hi[:, i % 2, :, :], kT[:, i % 2, :, :]).then_inc(kT_hi_ready, 1)

            def query_hi(b, j):
                act.wait_ge(q_turned, 4 * b + j + 1)
                wait_for(act, o_part, 4 * b + j - 1)
                act.copy(q_hi[:, j % 2, :], flat(f"QT{j}")).then_inc(q_hi_ready, 1)

            def exp_queries(b, p, i):
                act.wait_ge(q_shifted, 4 * b + i + 1)
                v = eq[:, p, 2 * i:2 * i + 2, :]
                act.activation(v, v, ACT.Exp).then_inc(q_exp, 1)

            def exp_keys(b, p, i):
                act.wait_ge(k_min_ready, 4 * b + i + 1)
                act.activation(ek[:, p, i, :], flat(f"K{i}"), ACT.Exp, bias=k_min[:, p, i:i + 1], scale=-1.0,
                               accum_out=k_sum[:, p, i:i + 1]).then_inc(k_exp, 1)

            def output(b, p):
                act.wait_ge(o_part, 4 * b + 4)
                if not isinstance(b, int) or b >= 2:
                    act.wait_ge(o_stored[p], 8 * (b - p))
                act.activation(o_sb[:, p, :], acc_flat, ACT.Identity, bias=w["bias"][:, 0:1],
                               scale=1.0).then_inc(o_copied, 1)

            def weighted_hi(b):
                act.wait_ge(t_part, 4 * b + 4)
                wait_for(act, m_made, b)
                act.copy(t_hi[:, :], acc[:, 0]).then_inc(t_hi_ready, 1)

            def folded_hi(b):
                act.wait_ge(m_scaled, 2 * b + 2)
                wait_for(act, o_part, 4 * b)
                act.copy(m_hi[:, :, :], m_full[:, :, :]).then_inc(m_hi_ready, 1)

            def norm_x(b, p):
                act.wait_ge(shift_ready, b + 1)
                wait_for(act, xn_lo_ready, b)
                act.activation(xn[:, :], x_sb[:, p, :], ACT.Identity, bias=shift[:, 0:1],
                               scale=rstd[:, 0:1]).then_inc(xn_ready, 1)

            def x_hi(b, p):
                act.wait_ge(xn_ready, b + 1)
                wait_for(act, q_made, 4 * (b - 1))
                act.copy(xn_hi[:, p, :], xn[:, :]).then_inc(xn_hi_ready, 1)

            def context_turned_hi(b):
                act.wait_ge(c_turned, b + 1)
                wait_for(act, t_part, 4 * b)
                act.copy(cT_hi[:, :, :].rearrange("p a b -> p (a b)"), flat("C0")).then_inc(cT_hi_ready, 1)

            def step(s, par, edge):
                X_, K, Q, C, KT, M, QT, O = (on(k, s, edge) for k in STAGES)
                if KT:
                    keys_copy(s - 1, 0)
                    keys_hi(s - 1, 0)
                if O:
                    output(s - 2, par)
                if KT:
                    keys_copy(s - 1, 1)
                if Q:
                    exp_queries(s, par, 0)
                if KT:
                    keys_hi(s - 1, 1)
                    keys_copy(s - 1, 2)
                if K:
                    exp_keys(s, par, 0)
                if KT:
                    keys_hi(s - 1, 2)
                    keys_copy(s - 1, 3)
                if Q:
                    exp_queries(s, par, 1)
                if KT:
                    keys_hi(s - 1, 3)
                if K:
                    exp_keys(s, par, 1)
                if QT:
                    query_hi(s - 1, 0)
                if KT:
                    weighted_hi(s - 1)
                if Q:
                    exp_queries(s, par, 2)
                if K:
                    exp_keys(s, par, 2)
                if M:
                    folded_hi(s - 1)
                if X_:
                    norm_x(s + 1, 1 - par)
                if QT:
                    query_hi(s - 1, 1)
                if X_:
                    x_hi(s + 1, 1 - par)
                if QT:
                    query_hi(s - 1, 2)
                if Q:
                    exp_queries(s, par, 3)
                if QT:
                    query_hi(s - 1, 3)
                if K:
                    exp_keys(s, par, 3)
                if C:
                    context_turned_hi(s)

            each_step(act, step)

        @block.vector
        def _(dve):
            def query_lo(b, j):
                dve.wait_ge(q_hi_ready, 4 * b + j + 1)
                dve.tensor_tensor(q_lo[:, j % 2, :], flat(f"QT{j}"), q_hi[:, j % 2, :].bitcast(F32),
                                  ALU.subtract).then_inc(q_lo_ready, 1)

            def shift_queries(b, p, i):
                dve.wait_ge(q_made, 4 * b + i + 1)
                src = flat(f"Q{i}").rearrange("p (g d) -> p g d", d=DH)
                dve.tensor_reduce(q_max[:, i, :], src, X, ALU.max).then_inc(q_max_ready, 1)
                dve.wait_ge(q_max_ready, 4 * b + i + 1)
                dst = eq[:, p, 2 * i:2 * i + 2, :].rearrange("p n (h d) -> p (n h) d", d=DH)
                dve.tensor_tensor(dst, src, per_row(q_max[:, i, :], 2 * HEADS, DH),
                                  ALU.subtract).then_inc(q_shifted, 1)

            def sum_queries(b, p, i):
                dve.wait_ge(q_exp, 4 * b + i + 1)
                v = eq[:, p, 2 * i:2 * i + 2, :].rearrange("p n (h d) -> p (n h) d", d=DH)
                dve.tensor_reduce(q_sum[:, i, :], v, X, ALU.add).then_inc(q_summed, 1)
                dve.wait_ge(q_summed, 4 * b + i + 1)
                wait_for(dve, q_normed, 4 * b + i - 3)
                dve.reciprocal(q_inv[:, i, :], q_sum[:, i, :]).then_inc(q_inv_ready, 1)

            def min_keys(b, p, i):
                dve.wait_ge(k_made, 4 * b + i + 1)
                dve.tensor_reduce(k_min[:, p, i:i + 1], flat(f"K{i}"), X, ALU.min).then_inc(k_min_ready, 1)

            def stats_x(b, p):
                dve.wait_ge(x_loaded[p], 8 * (b - p) + 16)
                for h in range(2):
                    dve.bn_stats(stats[:, h, :], x_sb[:, p, h * BANK:(h + 1) * BANK]).then_inc(x_stats, 1)
                dve.drain()
                dve.bn_aggr(mv[:, :], stats[:, :, :]).then_inc(x_mean_ready, 1)
                dve.wait_ge(x_mean_ready, b + 1)
                wait_for(dve, rstd_ready, b)
                dve.tensor_scalar(veps[:, :], mv[:, 1:2], EPS, None, ALU.add).then_inc(veps_ready, 1)

            def shift_x(b):
                dve.wait_ge(rstd_ready, b + 1)
                wait_for(dve, xn_ready, b)
                dve.scalar_tensor_tensor(out=shift[:, :], in0=mv[:, 0:1], scalar=-1.0, in1=rstd[:, :],
                                         op0=ALU.mult, op1=ALU.mult).then_inc(shift_ready, 1)

            def scale_m(b, p):
                dve.wait_ge(k_exp, 4 * b + 4)
                dve.reciprocal(k_inv[:, :], k_sum[:, p, :]).then_inc(k_inv_ready, 1)
                dve.wait_ge(k_inv_ready, b + 1)
                dve.wait_ge(m_made, b + 1)
                wait_for(dve, m_lo_ready, b)
                made = flat("M0").rearrange("p (j h c) -> p j h c", j=CH, h=2)
                for h in range(2):
                    r = slice(h * DH, (h + 1) * DH)
                    dve.scalar_tensor_tensor(out=m_full[r, :, :], in0=made[r, :, h, :], scalar=DH ** -0.5,
                                             in1=per_row(k_inv[r, :], CH, P), op0=ALU.mult,
                                             op1=ALU.mult).then_inc(m_scaled, 1)

            def weighted_lo(b):
                dve.wait_ge(t_hi_ready, b + 1)
                dve.tensor_tensor(t_lo[:, :], acc[:, 0], t_hi[:, :].bitcast(F32), ALU.subtract).then_inc(t_lo_ready, 1)

            def folded_lo(b):
                dve.wait_ge(m_hi_ready, b + 1)
                dve.tensor_tensor(m_lo[:, :, :], m_full[:, :, :], m_hi[:, :, :].bitcast(F32),
                                  ALU.subtract).then_inc(m_lo_ready, 1)

            def context_turned_lo(b):
                dve.wait_ge(cT_hi_ready, b + 1)
                dve.tensor_tensor(cT_lo[:, :, :].rearrange("p a b -> p (a b)"), flat("C0"),
                                  cT_hi[:, :, :].rearrange("p a b -> p (a b)").bitcast(F32),
                                  ALU.subtract).then_inc(cT_lo_ready, 1)

            def step(s, par, edge):
                X_, K, Q, C, KT, M, QT, O = (on(k, s, edge) for k in STAGES)
                if Q:
                    shift_queries(s, par, 0)
                if KT:
                    sum_queries(s - 1, 1 - par, 3)
                if K:
                    min_keys(s, par, 0)
                if Q:
                    shift_queries(s, par, 1)
                    sum_queries(s, par, 0)
                if K:
                    min_keys(s, par, 1)
                if X_:
                    stats_x(s + 1, 1 - par)
                if Q:
                    shift_queries(s, par, 2)
                if QT:
                    query_lo(s - 1, 0)
                if KT:
                    weighted_lo(s - 1)
                if K:
                    min_keys(s, par, 2)
                if M:
                    scale_m(s - 1, 1 - par)
                if X_:
                    shift_x(s + 1)
                if Q:
                    sum_queries(s, par, 1)
                if M:
                    folded_lo(s - 1)
                if QT:
                    query_lo(s - 1, 1)
                if Q:
                    shift_queries(s, par, 3)
                if QT:
                    query_lo(s - 1, 2)
                if K:
                    min_keys(s, par, 3)
                if QT:
                    query_lo(s - 1, 3)
                if Q:
                    sum_queries(s, par, 2)
                if C:
                    context_turned_lo(s)

            each_step(dve, step)

        @block.tensor
        def _(pe):
            def keys(s, par, i, edge):
                wait_slot(pe, f"K{i}", s, edge)
                if i == 0:
                    pe.wait_ge(ctx_lo_ready, s + 1)
                out = slot(f"K{i}")
                for n in range(2):
                    c = slice(n * BANK, (n + 1) * BANK)
                    last = split_products(pe, out[:, n], w["k_hi"][:, i * P:(i + 1) * P], w["k_lo"][:, i * P:(i + 1) * P],
                                          ctx_hi[:, par, c], ctx_lo[:, par, c], True, True)
                last.then_inc(k_made, 1)

            def queries(s, par, i, edge):
                wait_slot(pe, f"Q{i}", s, edge)
                if i == 0:
                    pe.wait_ge(xn_lo_ready, s + 1)
                out = slot(f"Q{i}")
                for n in range(2):
                    c = slice((2 * i + n) * P, (2 * i + n + 1) * P)
                    last = split_products(pe, out[:, n], xn_hi[:, par, c], xn_lo[:, par, c],
                                          w["q_hi"][:, :], w["q_lo"][:, :], True, True)
                last.then_inc(q_made, 1)

            def turn_query(s, par, j, edge):
                wait_slot(pe, f"QT{j}", s, edge)
                pe.wait_ge(q_normed, 4 * (s - 1) + 4)
                out = flat(f"QT{j}")
                for n in range(NCH):
                    last = pe.transpose(out[:, n * P:(n + 1) * P], eq[:, 1 - par, n, j * P:(j + 1) * P], ident[:, :])
                last.then_inc(q_turned, 1)

            def turn_keys(s, par, i, edge):
                wait_slot(pe, f"KT{i}", s, edge)
                pe.wait_ge(k_exp, 4 * (s - 1) + 4)
                out = slot(f"KT{i}")
                for n in range(2):
                    for j in range(CH):
                        c = (2 * i + n) * P
                        last = pe.transpose(out[:, n, j * P:(j + 1) * P], ek[:, 1 - par, j, c:c + P], ident[:, :])
                last.then_inc(kT_turned, 1)

            def turn_context(s, par, edge):
                wait_slot(pe, "C0", s, edge)
                pe.wait_ge(ctx_loaded[par], 8 * (s - par) + 16)
                out = flat("C0")
                for n in range(NCH):
                    last = pe.transpose(out[:, n * P:(n + 1) * P], ctx_sb[:, par, n * P:(n + 1) * P], ident[:, :])
                last.then_inc(c_turned, 1)

            def add_output(b, j):
                pe.wait_ge(q_lo_ready, 4 * b + j + 1)
                if j == 0:
                    pe.wait_ge(m_lo_ready, b + 1)
                    pe.wait_ge(t_lo_ready, b + 1)
                for n in range(2):
                    c = slice(n * BANK, (n + 1) * BANK)
                    last = split_products(pe, acc[:, n], m_hi[:, j, :], m_lo[:, j, :], q_hi[:, j % 2, c],
                                          q_lo[:, j % 2, c], j == 0, j == CH - 1)
                last.then_inc(o_part, 1)

            def add_weighted(b, i):
                pe.wait_ge(kT_lo_ready, 4 * b + i + 1)
                if i == 0:
                    pe.wait_ge(cT_lo_ready, b + 1)
                    wait_for(pe, o_copied, b)
                for n in range(2):
                    last = split_products(pe, acc[:, 0], cT_hi[:, 2 * i + n, :], cT_lo[:, 2 * i + n, :],
                                          kT_hi[:, i % 2, n, :], kT_lo[:, i % 2, n, :],
                                          i == 0 and n == 0, i == CH - 1 and n == 1)
                last.then_inc(t_part, 1)

            def fold(s, edge):
                wait_slot(pe, "M0", s, edge)
                pe.wait_ge(t_lo_ready, s - 1 + 1)
                for j in range(CH):
                    out = flat("M0")[:, 2 * j * P:2 * (j + 1) * P]
                    c, z = slice(j * P, (j + 1) * P), slice(2 * j * P, 2 * (j + 1) * P)
                    last = split_products(pe, out, t_hi[:, c], t_lo[:, c], w["z_hi"][:, z], w["z_lo"][:, z], True, True)
                last.then_inc(m_made, 1)

            def step(s, par, edge):
                X_, K, Q, C, KT, M, QT, O = (on(k, s, edge) for k in STAGES)
                if KT:
                    turn_keys(s, par, 0, edge)
                if Q:
                    queries(s, par, 0, edge)
                if O:
                    add_output(s - 2, 3)
                if KT:
                    turn_keys(s, par, 1, edge)
                if K:
                    keys(s, par, 0, edge)
                if KT:
                    turn_keys(s, par, 2, edge)
                if Q:
                    queries(s, par, 1, edge)
                if KT:
                    add_weighted(s - 1, 0)
                    turn_keys(s, par, 3, edge)
                if K:
                    keys(s, par, 1, edge)
                if KT:
                    add_weighted(s - 1, 1)
                if Q:
                    queries(s, par, 2, edge)
                if KT:
                    add_weighted(s - 1, 2)
                if QT:
                    turn_query(s, par, 0, edge)
                if KT:
                    add_weighted(s - 1, 3)
                if K:
                    keys(s, par, 2, edge)
                if M:
                    fold(s, edge)
                if QT:
                    turn_query(s, par, 1, edge)
                if Q:
                    queries(s, par, 3, edge)
                if QT:
                    turn_query(s, par, 2, edge)
                    add_output(s - 1, 0)
                if K:
                    keys(s, par, 3, edge)
                if QT:
                    add_output(s - 1, 1)
                    turn_query(s, par, 3, edge)
                if C:
                    turn_context(s, par, edge)
                if QT:
                    add_output(s - 1, 2)

            each_step(pe, step)


def mix_weights(nc, ident, ps, w, A, B, Wr):
    RAW = 4
    with ExitStack() as ctx:
        def sem(name):
            return ctx.enter_context(nc.semaphore(name))

        raw = ctx.enter_context(nc.sbuf_tensor("raw", [P, RAW, N], F32))
        raw_loaded = [sem(f"raw_loaded{i}") for i in range(RAW)]
        b_rows = ctx.enter_context(nc.sbuf_tensor("b_rows", [P, 2, NCH, P], F32))
        b_ordered = sem("b_ordered")
        raw_turned, w_hi_ready, w_lo_ready = sem("raw_turned"), sem("w_hi_ready"), sem("w_lo_ready")
        a_v = A.rearrange("k r d -> (k r) d")
        JOBS = 2 * KCH + 1
        block = ctx.enter_context(nc.Block())

        def part(which, n):
            if n < KCH:
                return w[f"a_{which}"][:, :, n * P:(n + 1) * P]
            if n < 2 * KCH:
                return w[f"b_{which}"][:, n - KCH, :].rearrange("q (p j) -> q j p", j=NCH)
            return w[f"r_{which}"][:, :, :]

        def turned(n):
            width = P if n < 2 * KCH else EXPERTS
            return ps[:, n % 4].rearrange("p a (b c) -> p (a b) c", c=P)[:, :, 0:width]

        @block.sync
        def _(sp):
            for n in range(JOBS):
                if n >= RAW:
                    sp.wait_ge(raw_turned, n - RAW + 1)
                    wait_for(sp, b_ordered, n - RAW + 1 - KCH)
                dst = raw[:, n % RAW, :]
                if n < KCH:
                    src = a_v[n * P:(n + 1) * P, :]
                elif n < 2 * KCH:
                    src = B[(n - KCH) * 8:(n - KCH + 1) * 8].rearrange("k (p j) r -> p k (j r)", j=NCH)
                    dst = dst.rearrange("p (k m) -> p k m", k=8)
                else:
                    src, dst = Wr, dst[0:EXPERTS, :]
                sp.dma_start(dst, src).then_inc(raw_loaded[n % RAW], 16)

        @block.gpsimd
        def _(pool):
            for m in range(KCH):
                n = KCH + m
                pool.wait_ge(raw_loaded[n % RAW], 16 * (n // RAW + 1))
                if m >= 2:
                    pool.wait_ge(raw_turned, n - 2 + 1)
                pool.tensor_scalar(b_rows[:, m % 2, :, :].rearrange("p j (k r) -> p k j r", k=8),
                                   raw[:, n % RAW, :].rearrange("p (k j r) -> p k j r", k=8, j=NCH), 1.0, None,
                                   ALU.mult).then_inc(b_ordered, 1)

        @block.tensor
        def _(pe):
            for n in range(JOBS):
                if KCH <= n < 2 * KCH:
                    pe.wait_ge(b_ordered, n - KCH + 1)
                else:
                    pe.wait_ge(raw_loaded[n % RAW], 16 * (n // RAW + 1))
                if n >= 4:
                    pe.wait_ge(w_lo_ready, n - 4 + 1)
                for m in range(NCH):
                    if n < KCH:
                        src = raw[:, n % RAW, m * P:(m + 1) * P]
                    elif n < 2 * KCH:
                        src = b_rows[:, n % 2, m, :]
                    else:
                        src = raw[0:EXPERTS, n % RAW, m * P:(m + 1) * P]
                    k = src.shape[0]
                    last = pe.transpose(turned(n)[:, m, :], src, ident[0:k, 0:k])
                last.then_inc(raw_turned, 1)

        @block.scalar
        def _(act):
            for n in range(JOBS):
                act.wait_ge(raw_turned, n + 1)
                act.copy(part("hi", n), turned(n)).then_inc(w_hi_ready, 1)

        @block.vector
        def _(dve):
            for n in range(JOBS):
                dve.wait_ge(w_hi_ready, n + 1)
                dve.tensor_tensor(part("lo", n), turned(n), part("hi", n).bitcast(F32),
                                  ALU.subtract).then_inc(w_lo_ready, 1)


def expert_mix(nc, ident, ps, w, x, o_dram, out):
    with ExitStack() as ctx:
        def sb(name, shape, dt=F32):
            return ctx.enter_context(nc.sbuf_tensor(name, shape, dt))

        def sem(name):
            return ctx.enter_context(nc.semaphore(name))

        x_sb = sb("x2_in", [P, 2, N])
        o_sb = sb("o_in", [P, 2, N])
        x2 = sb("x2", [P, 2, N])
        sq = sb("sq", [P, N])
        y = sb("y", [P, N])
        xn = sb("xn2", [P, N])
        xT_hi = sb("xT_hi", [P, NCH, P], F32R)
        xT_lo = sb("xT_lo", [P, NCH, P], F32R)
        hg = sb("hg", [P, KR])
        hT_hi = sb("hT_hi", [P, KCH, P], F32R)
        hT_lo = sb("hT_lo", [P, KCH, P], F32R)
        var_c = sb("var_c", [P, NCH])
        rstd_c = sb("rstd_c", [P, NCH])
        stats = sb("stats2", [P, 2, 6])
        mv = sb("mv2", [P, 2])
        veps = sb("veps2", [P, 1])
        rstd = sb("rstd2", [P, 1])
        shift = sb("shift2", [P, 1])
        score = sb("score", [P, EXPERTS])
        top = sb("top", [P, 2, 8])
        neg_top = sb("neg_top", [P, 1])
        rest = sb("rest", [P, 2, EXPERTS])
        e_all = sb("e_all", [P, EXPERTS])
        e_rest = sb("e_rest", [P, EXPERTS])
        gate_sum = sb("gate_sum", [P, 1])
        gate_inv = sb("gate_inv", [P, 1])
        gate_raw = sb("gate_raw", [P, EXPERTS])
        gate = sb("gate", [P, EXPERTS])

        x_loaded = [sem(f"x2_loaded{i}") for i in range(2)]
        o_loaded = [sem(f"o_loaded{i}") for i in range(2)]
        stored = [sem(f"stored{i}") for i in range(2)]
        o_turned, y_turned, x_turned, scored = sem("o_turned"), sem("y_turned"), sem("x_turned"), sem("scored")
        h_made, h_turned, r_made = sem("h_made"), sem("h_turned"), sem("r_made")
        squared, xn_ready, x_hi_ready, h_hi_ready = sem("squared"), sem("xn2_ready"), sem("x_hi_ready"), sem("h_hi_ready")
        scores_copied, e_all_ready, e_rest_ready = sem("scores_copied"), sem("e_all_ready"), sem("e_rest_ready")
        var_sum, var_ready, y_ready, x2_ready = sem("var_sum"), sem("var_ready"), sem("y_ready"), sem("x2_ready")
        x2_stats, x2_mean, veps_ready, shift_ready = sem("x2_stats"), sem("x2_mean"), sem("veps2_ready"), sem("shift_ready")
        rstd_c_ready, rstd_ready = sem("rstd_c_ready"), sem("rstd2_ready")
        x_lo_ready, h_lo_ready, h_gated, added = sem("x_lo_ready"), sem("h_lo_ready"), sem("h_gated"), sem("added")
        top_step, neg_top_ready, gate_step, gates_ready = sem("top_step"), sem("neg_top_ready"), sem("gate_step"), sem("gates_ready")

        ring = [ps[:, 0], ps[:, 1]]
        OT, YT, XT, SC = ring[0], ring[1], ring[1], ring[1][:, 0, 0:EXPERTS]
        HT = ring[0][:, 0]
        H, R = ps[:, 2], ps[:, 3]
        flat = "p a b -> p (a b)"

        def each_step(eng, step):
            for t in (-1, 0, 1, 2):
                step(t, t % 2, t >= 0, True)
            with eng.Fori(0, (BATCHES - 4) // 2) as i:
                for k in range(2):
                    step(2 * i + 3 + k, (3 + k) % 2, True, True)
            step(BATCHES - 1, (BATCHES - 1) % 2, True, False)

        block = ctx.enter_context(nc.Block())

        @block.sync
        def _(sp):
            def load(b, p):
                wait_for(sp, o_turned, b - 1)
                sp.dma_start(o_sb[:, p, :], o_dram[b]).then_inc(o_loaded[p], 16)
                wait_for(sp, x2_ready, b - 1)
                sp.dma_start(x_sb[:, p, :], x[b]).then_inc(x_loaded[p], 16)

            def step(t, par, mix, ahead):
                if ahead and (not isinstance(t, int) or t + 2 < BATCHES):
                    load_ok = True
                    load(t + 2, par)
                if mix:
                    sp.wait_ge(added, t + 1)
                    sp.dma_start(out[t], x2[:, par, :]).then_inc(stored[par], 16)

            load(0, 0)
            for t in (-1, 0, 1, 2):
                step(t, t % 2, t >= 0, True)
            with sp.Fori(0, (BATCHES - 4) // 2 - 1) as i:
                for k in range(2):
                    step(2 * i + 3 + k, (3 + k) % 2, True, True)
            for t in range(BATCHES - 3, BATCHES):
                step(t, t % 2, True, True)
            for sem_ in stored:
                sp.wait_ge(sem_, 16 * BATCHES // 2)

        @block.gpsimd
        def _(pool):
            def step(t, par, mix, ahead):
                if ahead:
                    b = t + 1
                    pool.wait_ge(var_ready, b + 1)
                    wait_for(pool, y_ready, b)
                    pool.tensor_tensor(rstd_c[:, :], var_c[:, :], w["minus_half"][:, 0:1].broadcast_to([P, NCH]),
                                       ALU.pow).then_inc(rstd_c_ready, 1)
                    pool.wait_ge(veps_ready, b + 1)
                    wait_for(pool, xn_ready, b)
                    pool.tensor_tensor(rstd[:, :], veps[:, :], w["minus_half"][:, :], ALU.pow).then_inc(rstd_ready, 1)

            each_step(pool, step)

        @block.scalar
        def _(act):
            def turned_hidden(t, half):
                act.wait_ge(h_turned, 2 * t + half + 1)
                if half == 0:
                    wait_for(act, r_made, t)
                dst = hT_hi[:, half * 4:half * 4 + 4, :].rearrange(flat)
                act.copy(dst, HT).then_inc(h_hi_ready, 1)

            def step(t, par, mix, ahead):
                b = t + 1
                if ahead:
                    act.wait_ge(o_turned, b + 1)
                    wait_for(act, var_sum, b)
                    act.activation(sq[:, :], OT.rearrange(flat), ACT.Square).then_inc(squared, 1)
                if mix:
                    turned_hidden(t, 0)
                if ahead:
                    act.wait_ge(shift_ready, b + 1)
                    wait_for(act, x_turned, b)
                    act.activation(xn[:, :], x2[:, 1 - par, :], ACT.Identity, bias=shift[:, 0:1],
                                   scale=rstd[:, 0:1]).then_inc(xn_ready, 1)
                    act.wait_ge(x_turned, b + 1)
                    wait_for(act, h_made, 2 * b)
                    act.copy(xT_hi[:, :, :].rearrange(flat), XT.rearrange(flat)).then_inc(x_hi_ready, 1)
                if mix:
                    turned_hidden(t, 1)
                if ahead:
                    act.wait_ge(neg_top_ready, b + 1)
                    wait_for(act, gate_step, 3 * b)
                    act.activation(e_all[:, :], score[:, :], ACT.Exp, bias=neg_top[:, 0:1],
                                   scale=1.0).then_inc(e_all_ready, 1)
                    act.wait_ge(top_step, 2 * b + 2)
                    act.activation(e_rest[:, :], rest[:, 1, :], ACT.Exp, bias=neg_top[:, 0:1],
                                   scale=1.0).then_inc(e_rest_ready, 1)

            each_step(act, step)

        @block.vector
        def _(dve):
            def gate_hidden(t, half):
                dve.wait_ge(h_made, 2 * t + half + 1)
                if half == 0:
                    dve.wait_ge(gates_ready, t + 1)
                wait_for(dve, h_turned, 2 * (t - 1) + half + 1)
                g0 = half * EXPERTS // 2
                v = hg[:, half * BANK:(half + 1) * BANK].rearrange("p (k r) -> p k r", r=RANK)
                dve.tensor_tensor(v, H[:, half].rearrange("p (k r) -> p k r", r=RANK),
                                  per_row(gate[:, g0:g0 + EXPERTS // 2], EXPERTS // 2, RANK),
                                  ALU.mult).then_inc(h_gated, 1)

            def turned_hidden(t, half):
                dve.wait_ge(h_hi_ready, 2 * t + half + 1)
                c = slice(half * 4, half * 4 + 4)
                dve.tensor_tensor(hT_lo[:, c, :].rearrange(flat), HT, hT_hi[:, c, :].rearrange(flat).bitcast(F32),
                                  ALU.subtract).then_inc(h_lo_ready, 1)

            def gates(b):
                dve.wait_ge(scored, b + 1)
                wait_for(dve, e_all_ready, b)
                dve.tensor_copy(score[:, :], SC).then_inc(scores_copied, 1)
                dve.drain()
                dve.max(top[:, 0, :], score[:, :]).then_inc(top_step, 1)
                dve.wait_ge(top_step, 2 * b + 1)
                wait_for(dve, e_rest_ready, b)
                dve.tensor_scalar(neg_top[:, :], top[:, 0, 0:1], -1.0, None, ALU.mult).then_inc(neg_top_ready, 1)
                dve.match_replace(rest[:, 0, :], top[:, 0, :], score[:, :], LOWEST)
                dve.drain()
                dve.max(top[:, 1, :], rest[:, 0, :])
                dve.drain()
                dve.match_replace(rest[:, 1, :], top[:, 1, :], rest[:, 0, :], LOWEST).then_inc(top_step, 1)
                dve.wait_ge(e_all_ready, b + 1)
                dve.wait_ge(e_rest_ready, b + 1)
                dve.tensor_tensor(gate_raw[:, :], e_all[:, :], e_rest[:, :], ALU.subtract).then_inc(gate_step, 1)
                dve.wait_ge(gate_step, 3 * b + 1)
                dve.tensor_reduce(gate_sum[:, :], gate_raw[:, :], X, ALU.add).then_inc(gate_step, 1)
                dve.wait_ge(gate_step, 3 * b + 2)
                dve.reciprocal(gate_inv[:, :], gate_sum[:, :]).then_inc(gate_step, 1)
                dve.wait_ge(gate_step, 3 * b + 3)
                dve.tensor_scalar(gate[:, :], gate_raw[:, :], gate_inv[:, 0:1], MIX_SCALE, ALU.mult,
                                  ALU.mult).then_inc(gates_ready, 1)

            def step(t, par, mix, ahead):
                b, p = t + 1, 1 - par
                if ahead:
                    dve.wait_ge(squared, b + 1)
                    dve.tensor_reduce(var_c[:, :], sq[:, :].rearrange("p (n c) -> p n c", c=P), X,
                                      ALU.add).then_inc(var_sum, 1)
                    dve.wait_ge(var_sum, b + 1)
                    dve.tensor_scalar(var_c[:, :], var_c[:, :], 1.0 / P, EPS, ALU.mult, ALU.add).then_inc(var_ready, 1)
                    dve.wait_ge(rstd_c_ready, b + 1)
                    wait_for(dve, y_turned, b)
                    dve.tensor_tensor(y[:, :].rearrange("p (n c) -> p n c", c=P),
                                      OT.rearrange("p a (b c) -> p (a b) c", c=P), per_row(rstd_c[:, :], NCH, P),
                                      ALU.mult).then_inc(y_ready, 1)
                if mix:
                    gate_hidden(t, 0)
                if ahead:
                    dve.wait_ge(y_turned, b + 1)
                    dve.wait_ge(x_loaded[p], 8 * (b - p) + 16)
                    if not isinstance(t, int) or b >= 2:
                        dve.wait_ge(stored[p], 8 * (b - p))
                    dve.scalar_tensor_tensor(out=x2[:, p, :], in0=YT.rearrange(flat), scalar=w["g"][:, 0:1],
                                             in1=x_sb[:, p, :], op0=ALU.mult, op1=ALU.add).then_inc(x2_ready, 1)
                    dve.wait_ge(x2_ready, b + 1)
                    for h in range(2):
                        dve.bn_stats(stats[:, h, :], x2[:, p, h * BANK:(h + 1) * BANK]).then_inc(x2_stats, 1)
                    dve.drain()
                    dve.bn_aggr(mv[:, :], stats[:, :, :]).then_inc(x2_mean, 1)
                    dve.wait_ge(x2_mean, b + 1)
                    dve.tensor_scalar(veps[:, :], mv[:, 1:2], EPS, None, ALU.add).then_inc(veps_ready, 1)
                    dve.wait_ge(rstd_ready, b + 1)
                    dve.scalar_tensor_tensor(out=shift[:, :], in0=mv[:, 0:1], scalar=-1.0, in1=rstd[:, :],
                                             op0=ALU.mult, op1=ALU.mult).then_inc(shift_ready, 1)
                if mix:
                    turned_hidden(t, 0)
                    gate_hidden(t, 1)
                if ahead:
                    dve.wait_ge(x_hi_ready, b + 1)
                    dve.tensor_tensor(xT_lo[:, :, :].rearrange(flat), XT.rearrange(flat),
                                      xT_hi[:, :, :].rearrange(flat).bitcast(F32), ALU.subtract).then_inc(x_lo_ready, 1)
                if mix:
                    turned_hidden(t, 1)
                if ahead:
                    gates(b)
                if mix:
                    dve.wait_ge(r_made, t + 1)
                    dve.tensor_tensor(x2[:, par, :], R.rearrange(flat), x2[:, par, :], ALU.add).then_inc(added, 1)

            each_step(dve, step)

        @block.tensor
        def _(pe):
            def turn(dst, src, done):
                for n in range(src.shape[1] // P):
                    last = pe.transpose(dst[:, n * P:(n + 1) * P], src[:, n * P:(n + 1) * P], ident[:, :])
                last.then_inc(done, 1)

            def hidden(half, chunks):
                for n in chunks:
                    last = split_products(pe, H[:, half], xT_hi[:, n, :], xT_lo[:, n, :],
                                          w["a_hi"][:, n, half * BANK:(half + 1) * BANK],
                                          w["a_lo"][:, n, half * BANK:(half + 1) * BANK], n == 0, n == NCH - 1)
                return last

            def result(chunks):
                for q in chunks:
                    for d in range(2):
                        last = split_products(pe, R[:, d], hT_hi[:, q, :], hT_lo[:, q, :],
                                              w["b_hi"][:, q, d * BANK:(d + 1) * BANK],
                                              w["b_lo"][:, q, d * BANK:(d + 1) * BANK], q == 0, q == KCH - 1)
                return last

            def step(t, par, mix, ahead):
                b, p = t + 1, 1 - par
                if ahead:
                    pe.wait_ge(o_loaded[p], 8 * (b - p) + 16)
                    wait_for(pe, h_lo_ready, 2 * t)
                    turn(OT.rearrange(flat), o_sb[:, p, :], o_turned)
                if mix:
                    pe.wait_ge(x_lo_ready, t + 1)
                    wait_for(pe, h_gated, 2 * t)
                    hidden(0, range(NCH)).then_inc(h_made, 1)
                if ahead:
                    pe.wait_ge(y_ready, b + 1)
                    wait_for(pe, scores_copied, b)
                    turn(YT.rearrange(flat), y[:, :], y_turned)
                if mix:
                    hidden(1, range(NCH // 2))
                    pe.wait_ge(h_gated, 2 * t + 1)
                    if not ahead:
                        pe.wait_ge(h_lo_ready, 2 * t)
                    turn(HT, hg[:, 0:BANK], h_turned)
                    hidden(1, range(NCH // 2, NCH)).then_inc(h_made, 1)
                if ahead:
                    pe.wait_ge(xn_ready, b + 1)
                    pe.wait_ge(x2_ready, b + 1)
                    turn(XT.rearrange(flat), xn[:, :], x_turned)
                if mix:
                    pe.wait_ge(h_lo_ready, 2 * t + 1)
                    wait_for(pe, added, t)
                    result(range(1))
                    pe.wait_ge(h_gated, 2 * t + 2)
                    turn(HT, hg[:, BANK:2 * BANK], h_turned)
                    result(range(1, KCH // 2))
                if ahead:
                    pe.wait_ge(x_lo_ready, b + 1)
                    for n in range(NCH):
                        last = split_products(pe, SC, xT_hi[:, n, :], xT_lo[:, n, :], w["r_hi"][:, n, :],
                                              w["r_lo"][:, n, :], n == 0, n == NCH - 1)
                    last.then_inc(scored, 1)
                if mix:
                    pe.wait_ge(h_lo_ready, 2 * t + 2)
                    result(range(KCH // 2, KCH)).then_inc(r_made, 1)

            each_step(pe, step)


def xattn_ffn(nc, x, context, Wq, Wkv, Wout, b_out, g, A, B, Wr, out):
    o_dram = nc.dram_tensor("attention_out", (BATCHES, P, N), F32).ap()
    with ExitStack() as ctx:
        def sb(name, shape, dt=F32):
            return ctx.enter_context(nc.sbuf_tensor(name, shape, dt))

        ps = ctx.enter_context(nc.psum_tensor("ps", [P, 4, 2, BANK], F32))
        ident = sb("ident", [P, P])
        w = {"g": sb("g_col", [P, 1]), "bias": sb("bias_col", [P, 1]), "minus_half": sb("minus_half", [P, 1]),
             "one": sb("one", [P, 1])}
        with ExitStack() as first:
            for name, width in (("q", HD), ("k", HD), ("z", 2 * HD)):
                for part in ("hi", "lo"):
                    w[f"{name}_{part}"] = first.enter_context(nc.sbuf_tensor(f"w_{name}_{part}", [P, width], F32R))
            attention_weights(nc, ident, ps, w, Wq, Wkv, Wout, b_out, g)
            attention(nc, ident, ps, w, x, context, o_dram)
        for part in ("hi", "lo"):
            w[f"a_{part}"] = sb(f"w_a_{part}", [P, NCH, KR], F32R)
            w[f"b_{part}"] = sb(f"w_b_{part}", [P, KCH, N], F32R)
            w[f"r_{part}"] = sb(f"w_r_{part}", [P, NCH, EXPERTS], F32R)
        mix_weights(nc, ident, ps, w, A, B, Wr)
        expert_mix(nc, ident, ps, w, x, o_dram, out)


_INS = ["x", "ctx_4096", "L0_xattn_Wq", "L0_xattn_Wkv", "L0_xattn_Wout", "L0_xattn_b_out", "L0_xattn_g",
        "L0_ffn_A", "L0_ffn_B", "L0_ffn_Wr"]


def kernel(**inputs):
    import numpy as _np
    import concourse.bacc as _bacc
    from concourse import mybir as _mybir
    from concourse.bass_utils import run_bass_kernel_spmd as _run

    nc = _bacc.Bacc("TRN2", target_bir_lowering=False, num_devices=1)
    arrays, args = {}, []
    for name in _INS:
        a = _np.ascontiguousarray(inputs[name])
        arrays[f"in_{name}"] = a
        args.append(nc.dram_tensor(f"in_{name}", a.shape, _mybir.dt.from_np(a.dtype), kind="ExternalInput").ap())
    args.append(nc.dram_tensor("out_0", (BATCHES, P, N), F32, kind="ExternalOutput").ap())
    xattn_ffn(nc, *args)
    r = _run(nc, [arrays], core_ids=[0])
    return r.results[0]["out_0"]
```

```python
from contextlib import ExitStack

import concourse.bass as bass
from concourse import mybir

F32 = mybir.dt.float32
F32R = mybir.dt.float32r
ALU = mybir.AluOpType
ACT = mybir.ActivationFunctionType
X = mybir.AxisListType.X

P = 128
BANK = 512
BATCHES, N = 32, 1024
HEADS, DH = 8, 64
HD = HEADS * DH
CH = HD // P
NCH = N // P
EXPERTS, RANK, TOPK = 64, 16, 16
KR = EXPERTS * RANK
KCH = KR // P
EPS = 1e-5
MIX_SCALE = 32.0 / RANK
LOWEST = -3.4028234e38


def wait_for(eng, sem, value):
    if isinstance(value, int) and value <= 0:
        return
    eng.wait_ge(sem, value)


def per_row(col, groups, width):
    return col.unsqueeze(2).broadcast_to([col.shape[0], groups, width])


def split_products(pe, out, stat_hi, stat_lo, mov_hi, mov_lo, first, last):
    pe.matmul(out, stat_hi, mov_hi, start=first, stop=False)
    pe.matmul(out, stat_hi, mov_lo, start=False, stop=False)
    return pe.matmul(out, stat_lo, mov_hi, start=False, stop=last)


RING = ["KT0", "Q0", "KT1", "K0", "KT2", "Q1", "KT3", "K1", "Q2",
        "QT0", "K2", "M0", "QT1", "Q3", "QT2", "K3", "QT3", "C0"]
SLOTS = 3
DELAY = {"X": -1, "K": 0, "C": 0, "Q": 0, "KT": 1, "M": 1, "QT": 1, "O": 2}
PER_BATCH = {"K": 4, "C": 1, "Q": 4, "KT": 4, "M": 1, "QT": 4}
FIRST_STEP, FULL_FROM, FULL_TO, STEPS = -1, 4, BATCHES - 2, BATCHES + 2


def attention(nc, ident, ps, w, shared, x, context, Wq, Wkv, Wout, b_out, g, Wr, o_dram):
    with ExitStack() as ctx:
        def sb(name, shape, dt=F32):
            return ctx.enter_context(nc.sbuf_tensor(name, shape, dt))

        def sem(name):
            return ctx.enter_context(nc.semaphore(name))

        wq_hi, wq_lo = sb("wq_hi", [P, HD], F32R), sb("wq_lo", [P, HD], F32R)
        wk_hi, wk_lo = sb("wk_hi", [P, HD], F32R), sb("wk_lo", [P, HD], F32R)
        z_hi, z_lo = sb("z_hi", [P, 2 * HD], F32R), sb("z_lo", [P, 2 * HD], F32R)

        x_sb, o_sb = shared["x_sb"], shared["o_sb"]
        ctx_sb = sb("ctx_sb", [P, 2, N])
        ctx_hi = sb("ctx_hi", [P, 2, N], F32R)
        ctx_lo = sb("ctx_lo", [P, 2, N], F32R)
        xn = sb("xn", [P, N])
        xn_hi = sb("xn_hi", [P, 2, N], F32R)
        xn_lo = sb("xn_lo", [P, 2, N], F32R)
        cT_hi = sb("cT_hi", [P, NCH, P], F32R)
        cT_lo = sb("cT_lo", [P, NCH, P], F32R)
        ek = sb("ek", [P, 2, CH, N])
        eq = sb("eq", [P, 2, NCH, HD])
        kT = sb("kT", [P, 2, 2, HD])
        kT_hi = sb("kT_hi", [P, 2, 2, HD], F32R)
        kT_lo = sb("kT_lo", [P, 2, 2, HD], F32R)
        q_hi = sb("qh", [P, 2, N], F32R)
        q_lo = sb("ql", [P, 2, N], F32R)
        t_hi = sb("t_hi", [P, HD], F32R)
        t_lo = sb("t_lo", [P, HD], F32R)
        m_full = sb("m_full", [P, CH, P])
        m_hi = sb("m_hi", [P, CH, P], F32R)
        m_lo = sb("m_lo", [P, CH, P], F32R)
        k_min = sb("k_min", [P, 2, CH])
        k_sum = sb("k_sum", [P, 2, CH])
        k_inv = sb("k_inv", [P, CH])
        q_max = sb("q_max", [P, 4, 2 * HEADS])
        q_sum = sb("q_sum", [P, 4, 2 * HEADS])
        q_inv = sb("q_inv", [P, 4, 2 * HEADS])
        stats = sb("stats", [P, 2, 6])
        mv = sb("mv", [P, 2])
        veps = sb("veps", [P, 1])
        rstd = sb("rstd", [P, 1])
        shift = sb("shift", [P, 1])

        wq_raw, wk_raw, wv_raw = (ek[:, 1, i, 0:HD].rearrange("p (j c) -> p j c", j=CH) for i in range(3))
        wo_raw, b_rows = ek[:, 1, 0, HD:2 * HD], ek[:, 1, 1, HD:HD + P]
        wo_pairs = ek[:, 1, 3, :].rearrange("p (j h c) -> p j h c", j=CH, h=2)
        b_col, b_mean = sb("b_col", [P, 1]), sb("b_mean", [P, 1])
        wo_sum, wo_mean = sb("wo_sum", [P, CH]), sb("wo_mean", [P, CH])
        wqT, wkT, woT, z_sum = ps[:, 0, 0], ps[:, 0, 1], ps[:, 2, 0], ps[:, 3].rearrange("p a b -> p (a b)")

        consts_set, ident_ready, pairs_zeroed = sem("consts_set"), sem("ident_ready"), sem("pairs_zeroed")
        qk_loaded, rest_loaded, qk_turned, wo_turned = sem("qk_loaded"), sem("rest_loaded"), sem("qk_turned"), sem("wo_turned")
        wo_step, b_step, wo_centred = sem("wo_step"), sem("b_step"), sem("wo_centred")
        qk_hi_ready, qk_lo_ready = sem("qk_hi_ready"), sem("qk_lo_ready")
        z_folded, z_hi_ready, z_lo_ready = sem("z_folded"), sem("z_hi_ready"), sem("z_lo_ready")

        ctx_loaded = [sem(f"ctx_loaded{i}") for i in range(2)]
        x_loaded = [sem(f"x_loaded{i}") for i in range(2)]
        o_stored = shared["o_stored"]
        k_made, c_turned, q_made = sem("k_made"), sem("c_turned"), sem("q_made")
        kT_turned, q_turned = sem("kT_turned"), sem("q_turned")
        t_part, m_made, o_part = sem("t_part"), sem("m_made"), sem("o_part")
        k_min_ready, q_max_ready, q_shifted = sem("k_min_ready"), sem("q_max_ready"), sem("q_shifted")
        q_summed, q_inv_ready = sem("q_summed"), sem("q_inv_ready")
        q_lo_ready, cT_lo_ready = sem("q_lo_ready"), sem("cT_lo_ready")
        t_lo_ready, k_inv_ready, m_scaled, m_lo_ready = (
            sem("t_lo_ready"), sem("k_inv_ready"), sem("m_scaled"), sem("m_lo_ready"))
        x_stats, x_mean_ready, veps_ready, shift_ready = (
            sem("x_stats"), sem("x_mean_ready"), sem("veps_ready"), sem("shift_ready"))
        k_exp, q_exp, q_hi_ready = sem("k_exp"), sem("q_exp"), sem("q_hi_ready")
        kT_copied, kT_hi_ready = sem("kT_copied"), sem("kT_hi_ready")
        cT_hi_ready, t_hi_ready, m_hi_ready, o_copied = (
            sem("cT_hi_ready"), sem("t_hi_ready"), sem("m_hi_ready"), sem("o_copied"))
        xn_ready, xn_hi_ready = sem("xn_ready"), sem("xn_hi_ready")
        kT_lo_ready, q_normed = sem("kT_lo_ready"), sem("q_normed")
        ctx_hi_ready, ctx_lo_ready = sem("ctx_hi_ready"), sem("ctx_lo_ready")
        rstd_ready, xn_lo_ready = sem("rstd_ready"), sem("xn_lo_ready")

        slot_read = {"K": k_exp, "C": cT_lo_ready, "Q": q_shifted, "KT": kT_copied, "M": m_scaled,
                     "QT": q_lo_ready}

        def slot(job):
            return ps[:, RING.index(job) % SLOTS]

        def flat(job):
            return slot(job).rearrange("p a b -> p (a b)")

        acc = ps[:, SLOTS]
        acc_flat = acc.rearrange("p a b -> p (a b)")

        def on(kind, s, edge):
            return not edge or 0 <= s - DELAY[kind] < BATCHES

        def wait_slot(eng, job, s, edge):
            n, back = RING.index(job), 0
            while True:
                n -= SLOTS
                if n < 0:
                    n, back = n + len(RING), back + 1
                kind, i = RING[n][:-1], int(RING[n][-1])
                if edge and s - back < 0:
                    return
                if on(kind, s - back, edge):
                    b = s - back - DELAY[kind]
                    wait_for(eng, slot_read[kind], 2 * b + 2 if kind == "M" else PER_BATCH[kind] * b + i + 1)
                    return

        def each_step(eng, step):
            for s in range(FIRST_STEP, FULL_FROM):
                step(s, s % 2, True)
            with eng.Fori(FULL_FROM // 2, FULL_TO // 2) as i:
                for parity in range(2):
                    step(2 * i + parity, parity, False)
            for s in range(FULL_TO, STEPS):
                step(s, s % 2, True)

        STAGES = ("X", "K", "Q", "C", "KT", "M", "QT", "O")
        block = ctx.enter_context(nc.Block())

        @block.sync
        def _(sp):
            def load_context(b, p):
                wait_for(sp, ctx_lo_ready, b - 1)
                wait_for(sp, c_turned, b - 1)
                sp.dma_start(ctx_sb[:, p, :], context[b]).then_inc(ctx_loaded[p], 16)

            def load_x(b, p):
                wait_for(sp, xn_ready, b - 1)
                sp.dma_start(x_sb[:, p, :], x[b]).then_inc(x_loaded[p], 16)

            def step(s, par, edge):
                if not edge or 0 <= s + 1 < BATCHES:
                    load_context(s + 1, 1 - par)
                if edge and s == FIRST_STEP:
                    for dst, src in ((wo_raw, Wout), (b_col[:, :], b_out.rearrange("(c a) -> c a", a=1)),
                                     (b_rows, b_out.rearrange("(a c) -> a c", a=1).broadcast_to([P, P])),
                                     (wv_raw, Wkv[HD:2 * HD, :].rearrange("(j p) c -> p j c", p=P)),
                                     (w["g"][:, :], g.rearrange("a c b -> (a c) b"))):
                        sp.dma_start(dst, src).then_inc(rest_loaded, 16)
                if not edge or 0 <= s + 2 < BATCHES:
                    load_x(s + 2, par)
                if edge and s == STEPS - 1:
                    sp.wait_ge(xn_ready, BATCHES)
                    sp.dma_start(x_sb[0:EXPERTS, 1, :], Wr).then_inc(shared["raw_loaded"][0], 16)
                    sp.dma_start(x_sb[:, 0, :], x[0]).then_inc(shared["x_loaded"][0], 16)
                    sp.wait_ge(o_stored[0], 16 * BATCHES // 2)
                    sp.dma_start(o_sb[:, 0, :], o_dram[0]).then_inc(shared["o_loaded"][0], 16)
                if on("O", s, edge):
                    sp.wait_ge(o_copied, s - 2 + 1)
                    sp.dma_start(o_dram[s - 2], o_sb[:, par, :]).then_inc(o_stored[par], 16)

            load_x(0, 0)
            sp.dma_start(wq_raw, Wq.rearrange("(j p) c -> p j c", p=P)).then_inc(qk_loaded, 16)
            sp.dma_start(wk_raw, Wkv[0:HD, :].rearrange("(j p) c -> p j c", p=P)).then_inc(qk_loaded, 16)
            each_step(sp, step)
        @block.gpsimd
        def _(pool):
            def rstd_x(b):
                pool.wait_ge(veps_ready, b + 1)
                wait_for(pool, xn_ready, b)
                pool.tensor_tensor(rstd[:, :], veps[:, :], w["minus_half"][:, :], ALU.pow).then_inc(rstd_ready, 1)

            def context_hi(b, p):
                pool.wait_ge(ctx_loaded[p], 8 * (b - p) + 16)
                wait_for(pool, k_made, CH * (b - 1))
                pool.tensor_tensor(ctx_hi[:, p, :], ctx_sb[:, p, :], w["one"][:, 0:1].broadcast_to([P, N]),
                                   ALU.mult).then_inc(ctx_hi_ready, 1)

            def context_lo(b, p):
                pool.wait_ge(ctx_hi_ready, b + 1)
                pool.tensor_tensor(ctx_lo[:, p, :], ctx_sb[:, p, :], ctx_hi[:, p, :].bitcast(F32),
                                   ALU.subtract).then_inc(ctx_lo_ready, 1)

            def x_lo(b, p):
                wait_for(pool, q_made, 4 * (b - 1))
                pool.wait_ge(xn_hi_ready, b + 1)
                pool.tensor_tensor(xn_lo[:, p, :], xn[:, :], xn_hi[:, p, :].bitcast(F32),
                                   ALU.subtract).then_inc(xn_lo_ready, 1)

            def norm_queries(b, p, i):
                pool.wait_ge(q_inv_ready, 4 * b + i + 1)
                v = eq[:, p, 2 * i:2 * i + 2, :].rearrange("p n (h d) -> p (n h) d", d=DH)
                pool.tensor_tensor(v, v, per_row(q_inv[:, i, :], 2 * HEADS, DH), ALU.mult).then_inc(q_normed, 1)

            def keys_lo(b, i):
                pool.wait_ge(kT_hi_ready, 4 * b + i + 1)
                pool.tensor_tensor(kT_lo[:, i % 2, :, :], kT[:, i % 2, :, :], kT_hi[:, i % 2, :, :].bitcast(F32),
                                   ALU.subtract).then_inc(kT_lo_ready, 1)

            def step(s, par, edge):
                X_, K, Q, C, KT, M, QT, O = (on(k, s, edge) for k in STAGES)
                if KT:
                    keys_lo(s - 1, 0)
                    keys_lo(s - 1, 1)
                    norm_queries(s - 1, 1 - par, 3)
                    keys_lo(s - 1, 2)
                    keys_lo(s - 1, 3)
                if X_:
                    rstd_x(s + 1)
                    context_hi(s + 1, 1 - par)
                if Q:
                    norm_queries(s, par, 0)
                if X_:
                    context_lo(s + 1, 1 - par)
                    x_lo(s + 1, 1 - par)
                if Q:
                    norm_queries(s, par, 1)
                    norm_queries(s, par, 2)

            pool.memset(w["minus_half"][:, :], -0.5).then_inc(consts_set, 1)
            pool.memset(w["one"][:, :], 1.0).then_inc(consts_set, 1)
            pool.memset(ident[:, :], 0.0).then_inc(consts_set, 1)
            pool.wait_ge(consts_set, 3)
            pool.affine_select(out=ident[:, :], in_=ident[:, :], compare_op=ALU.not_equal, fill=1.0,
                               base=0, pattern=[[-1, P]], channel_multiplier=1).then_inc(ident_ready, 1)
            pool.memset(wo_pairs, 0.0).then_inc(pairs_zeroed, 1)
            each_step(pool, step)

        @block.scalar
        def _(act):
            def keys_copy(b, i):
                act.wait_ge(kT_turned, 4 * b + i + 1)
                wait_for(act, kT_lo_ready, 4 * b + i - 1)
                act.copy(kT[:, i % 2, :, :], slot(f"KT{i}")).then_inc(kT_copied, 1)

            def keys_hi(b, i):
                act.wait_ge(kT_copied, 4 * b + i + 1)
                wait_for(act, t_part, 4 * b + i - 1)
                act.copy(kT_hi[:, i % 2, :, :], kT[:, i % 2, :, :]).then_inc(kT_hi_ready, 1)

            def query_hi(b, j):
                act.wait_ge(q_turned, 4 * b + j + 1)
                wait_for(act, o_part, 4 * b + j - 1)
                act.copy(q_hi[:, j % 2, :], flat(f"QT{j}")).then_inc(q_hi_ready, 1)

            def exp_queries(b, p, i):
                act.wait_ge(q_shifted, 4 * b + i + 1)
                v = eq[:, p, 2 * i:2 * i + 2, :]
                act.activation(v, v, ACT.Exp).then_inc(q_exp, 1)

            def exp_keys(b, p, i):
                act.wait_ge(k_min_ready, 4 * b + i + 1)
                act.activation(ek[:, p, i, :], flat(f"K{i}"), ACT.Exp, bias=k_min[:, p, i:i + 1], scale=-1.0,
                               accum_out=k_sum[:, p, i:i + 1]).then_inc(k_exp, 1)

            def output(b, p):
                act.wait_ge(o_part, 4 * b + 4)
                if isinstance(b, int) and b == 0:
                    act.wait_ge(b_step, 3)
                if not isinstance(b, int) or b >= 2:
                    act.wait_ge(o_stored[p], 8 * (b - p))
                act.activation(o_sb[:, p, :], acc_flat, ACT.Identity, bias=w["bias"][:, 0:1],
                               scale=1.0).then_inc(o_copied, 1)

            def weighted_hi(b):
                act.wait_ge(t_part, 4 * b + 4)
                wait_for(act, m_made, b)
                act.copy(t_hi[:, :], acc[:, 0]).then_inc(t_hi_ready, 1)

            def folded_hi(b):
                act.wait_ge(m_scaled, 2 * b + 2)
                wait_for(act, o_part, 4 * b)
                act.copy(m_hi[:, :, :], m_full[:, :, :]).then_inc(m_hi_ready, 1)

            def norm_x(b, p):
                act.wait_ge(shift_ready, b + 1)
                wait_for(act, xn_lo_ready, b)
                act.activation(xn[:, :], x_sb[:, p, :], ACT.Identity, bias=shift[:, 0:1],
                               scale=rstd[:, 0:1]).then_inc(xn_ready, 1)

            def x_hi(b, p):
                act.wait_ge(xn_ready, b + 1)
                wait_for(act, q_made, 4 * (b - 1))
                act.copy(xn_hi[:, p, :], xn[:, :]).then_inc(xn_hi_ready, 1)

            def context_turned_hi(b):
                act.wait_ge(c_turned, b + 1)
                wait_for(act, t_part, 4 * b)
                act.copy(cT_hi[:, :, :].rearrange("p a b -> p (a b)"), flat("C0")).then_inc(cT_hi_ready, 1)

            def step(s, par, edge):
                X_, K, Q, C, KT, M, QT, O = (on(k, s, edge) for k in STAGES)
                if edge and s == 1:
                    act.wait_ge(z_folded, 1)
                    act.copy(z_hi[:, :], z_sum).then_inc(z_hi_ready, 1)
                if KT:
                    keys_copy(s - 1, 0)
                    keys_hi(s - 1, 0)
                    keys_copy(s - 1, 1)
                    keys_hi(s - 1, 1)
                if O:
                    output(s - 2, par)
                if Q:
                    exp_queries(s, par, 0)
                if K:
                    exp_keys(s, par, 0)
                if KT:
                    keys_copy(s - 1, 2)
                    keys_hi(s - 1, 2)
                    keys_copy(s - 1, 3)
                    keys_hi(s - 1, 3)
                if K:
                    exp_keys(s, par, 1)
                if QT:
                    query_hi(s - 1, 0)
                if Q:
                    exp_queries(s, par, 1)
                if KT:
                    weighted_hi(s - 1)
                if K:
                    exp_keys(s, par, 2)
                if QT:
                    query_hi(s - 1, 1)
                if M:
                    folded_hi(s - 1)
                if Q:
                    exp_queries(s, par, 2)
                if QT:
                    query_hi(s - 1, 2)
                if X_:
                    norm_x(s + 1, 1 - par)
                    x_hi(s + 1, 1 - par)
                if QT:
                    query_hi(s - 1, 3)
                if K:
                    exp_keys(s, par, 3)
                if C:
                    context_turned_hi(s)
                if Q:
                    exp_queries(s, par, 3)

            each_step(act, step)

        @block.vector
        def _(dve):
            def weights():
                dve.wait_ge(qk_turned, 1)
                dve.tensor_copy(wq_hi[:, :], wqT).then_inc(qk_hi_ready, 1)
                dve.tensor_scalar(wk_hi[:, :], wkT, -1.0, None, ALU.mult).then_inc(qk_hi_ready, 1)
                dve.wait_ge(qk_hi_ready, 2)
                dve.tensor_tensor(wq_lo[:, :], wqT, wq_hi[:, :].bitcast(F32), ALU.subtract).then_inc(qk_lo_ready, 1)
                dve.scalar_tensor_tensor(out=wk_lo[:, :], in0=wkT, scalar=-1.0, in1=wk_hi[:, :].bitcast(F32),
                                         op0=ALU.mult, op1=ALU.subtract).then_inc(qk_lo_ready, 1)
                dve.wait_ge(wo_turned, 1)
                woT3 = woT.rearrange("p (j c) -> p j c", j=CH)
                dve.reduce_sum(wo_sum[:, :], woT3, axis=X).then_inc(wo_step, 1)
                dve.reduce_sum(b_mean[:, :], b_rows, axis=X).then_inc(b_step, 1)
                dve.wait_ge(wo_step, 1)
                dve.tensor_scalar(wo_mean[:, :], wo_sum[:, :], 1.0 / P, None, ALU.mult).then_inc(wo_step, 1)
                dve.wait_ge(b_step, 1)
                dve.tensor_scalar(b_mean[:, :], b_mean[:, :], 1.0 / P, None, ALU.mult).then_inc(b_step, 1)
                dve.wait_ge(wo_step, 2)
                dve.wait_ge(pairs_zeroed, 1)
                for h in range(2):
                    r = slice(h * DH, (h + 1) * DH)
                    dve.tensor_tensor(wo_pairs[r, :, h, :], woT3[r, :, :], per_row(wo_mean[r, :], CH, P),
                                      ALU.subtract).then_inc(wo_centred, 1)
                dve.wait_ge(b_step, 2)
                dve.tensor_tensor(w["bias"][:, :], b_col[:, :], b_mean[:, :], ALU.subtract).then_inc(b_step, 1)

            def query_lo(b, j):
                dve.wait_ge(q_hi_ready, 4 * b + j + 1)
                dve.tensor_tensor(q_lo[:, j % 2, :], flat(f"QT{j}"), q_hi[:, j % 2, :].bitcast(F32),
                                  ALU.subtract).then_inc(q_lo_ready, 1)

            def max_queries(b, i):
                dve.wait_ge(q_made, 4 * b + i + 1)
                src = flat(f"Q{i}").rearrange("p (g d) -> p g d", d=DH)
                dve.tensor_reduce(q_max[:, i, :], src, X, ALU.max).then_inc(q_max_ready, 1)

            def shift_queries(b, p, i):
                dve.wait_ge(q_max_ready, 4 * b + i + 1)
                src = flat(f"Q{i}").rearrange("p (g d) -> p g d", d=DH)
                dst = eq[:, p, 2 * i:2 * i + 2, :].rearrange("p n (h d) -> p (n h) d", d=DH)
                dve.tensor_tensor(dst, src, per_row(q_max[:, i, :], 2 * HEADS, DH),
                                  ALU.subtract).then_inc(q_shifted, 1)

            def sum_queries(b, p, i):
                dve.wait_ge(q_exp, 4 * b + i + 1)
                v = eq[:, p, 2 * i:2 * i + 2, :].rearrange("p n (h d) -> p (n h) d", d=DH)
                dve.tensor_reduce(q_sum[:, i, :], v, X, ALU.add).then_inc(q_summed, 1)

            def invert_sums(b, i):
                dve.wait_ge(q_summed, 4 * b + i + 1)
                wait_for(dve, q_normed, 4 * b + i - 3)
                dve.reciprocal(q_inv[:, i, :], q_sum[:, i, :]).then_inc(q_inv_ready, 1)

            def min_keys(b, p, i):
                dve.wait_ge(k_made, 4 * b + i + 1)
                dve.tensor_reduce(k_min[:, p, i:i + 1], flat(f"K{i}"), X, ALU.min).then_inc(k_min_ready, 1)

            def stats_x(b, p, h):
                dve.wait_ge(x_loaded[p], 8 * (b - p) + 16)
                dve.bn_stats(stats[:, h, :], x_sb[:, p, h * BANK:(h + 1) * BANK]).then_inc(x_stats, 1)

            def mean_x(b):
                dve.drain()
                dve.bn_aggr(mv[:, :], stats[:, :, :]).then_inc(x_mean_ready, 1)
                dve.wait_ge(x_mean_ready, b + 1)
                wait_for(dve, rstd_ready, b)
                dve.tensor_scalar(veps[:, :], mv[:, 1:2], EPS, None, ALU.add).then_inc(veps_ready, 1)

            def shift_x(b):
                dve.wait_ge(rstd_ready, b + 1)
                wait_for(dve, xn_ready, b)
                dve.scalar_tensor_tensor(out=shift[:, :], in0=mv[:, 0:1], scalar=-1.0, in1=rstd[:, :],
                                         op0=ALU.mult, op1=ALU.mult).then_inc(shift_ready, 1)

            def scale_m(b, p):
                dve.wait_ge(k_exp, 4 * b + 4)
                dve.reciprocal(k_inv[:, :], k_sum[:, p, :]).then_inc(k_inv_ready, 1)
                dve.wait_ge(k_inv_ready, b + 1)
                dve.wait_ge(m_made, b + 1)
                wait_for(dve, m_lo_ready, b)
                made = flat("M0").rearrange("p (j h c) -> p j h c", j=CH, h=2)
                for h in range(2):
                    r = slice(h * DH, (h + 1) * DH)
                    dve.scalar_tensor_tensor(out=m_full[r, :, :], in0=made[r, :, h, :], scalar=DH ** -0.5,
                                             in1=per_row(k_inv[r, :], CH, P), op0=ALU.mult,
                                             op1=ALU.mult).then_inc(m_scaled, 1)

            def weighted_lo(b):
                dve.wait_ge(t_hi_ready, b + 1)
                dve.tensor_tensor(t_lo[:, :], acc[:, 0], t_hi[:, :].bitcast(F32), ALU.subtract).then_inc(t_lo_ready, 1)

            def folded_lo(b):
                dve.wait_ge(m_hi_ready, b + 1)
                dve.tensor_tensor(m_lo[:, :, :], m_full[:, :, :], m_hi[:, :, :].bitcast(F32),
                                  ALU.subtract).then_inc(m_lo_ready, 1)

            def context_turned_lo(b):
                dve.wait_ge(cT_hi_ready, b + 1)
                dve.tensor_tensor(cT_lo[:, :, :].rearrange("p a b -> p (a b)"), flat("C0"),
                                  cT_hi[:, :, :].rearrange("p a b -> p (a b)").bitcast(F32),
                                  ALU.subtract).then_inc(cT_lo_ready, 1)

            def step(s, par, edge):
                X_, K, Q, C, KT, M, QT, O = (on(k, s, edge) for k in STAGES)
                if edge and s == 0:
                    weights()
                if edge and s == 1:
                    dve.wait_ge(z_hi_ready, 1)
                    dve.tensor_tensor(z_lo[:, :], z_sum, z_hi[:, :].bitcast(F32), ALU.subtract).then_inc(z_lo_ready, 1)
                if Q:
                    max_queries(s, 0)
                    shift_queries(s, par, 0)
                if K:
                    min_keys(s, par, 0)
                if KT:
                    sum_queries(s - 1, 1 - par, 3)
                    invert_sums(s - 1, 3)
                if Q:
                    max_queries(s, 1)
                if X_:
                    stats_x(s + 1, 1 - par, 0)
                if Q:
                    shift_queries(s, par, 1)
                if X_:
                    stats_x(s + 1, 1 - par, 1)
                if Q:
                    sum_queries(s, par, 0)
                if K:
                    min_keys(s, par, 1)
                if Q:
                    max_queries(s, 2)
                if X_:
                    mean_x(s + 1)
                if Q:
                    shift_queries(s, par, 2)
                if X_:
                    shift_x(s + 1)
                if QT:
                    query_lo(s - 1, 0)
                if KT:
                    weighted_lo(s - 1)
                if K:
                    min_keys(s, par, 2)
                if Q:
                    invert_sums(s, 0)
                if M:
                    scale_m(s - 1, 1 - par)
                if Q:
                    sum_queries(s, par, 1)
                if M:
                    folded_lo(s - 1)
                if QT:
                    query_lo(s - 1, 1)
                if Q:
                    max_queries(s, 3)
                    shift_queries(s, par, 3)
                if QT:
                    query_lo(s - 1, 2)
                if K:
                    min_keys(s, par, 3)
                if Q:
                    sum_queries(s, par, 2)
                if QT:
                    query_lo(s - 1, 3)
                if Q:
                    invert_sums(s, 1)
                if C:
                    context_turned_lo(s)
                if Q:
                    invert_sums(s, 2)

            each_step(dve, step)

        @block.tensor
        def _(pe):
            def turn_weights():
                pe.wait_ge(ident_ready, 1)
                pe.wait_ge(qk_loaded, 2 * 16)
                for dst, src in ((wqT, wq_raw), (wkT, wk_raw)):
                    for j in range(CH):
                        last = pe.transpose(dst[:, j * P:(j + 1) * P], src[:, j, :], ident[:, :])
                last.then_inc(qk_turned, 1)
                pe.wait_ge(rest_loaded, 5 * 16)
                for j in range(CH):
                    last = pe.transpose(woT[:, j * P:(j + 1) * P], wo_raw[:, j * P:(j + 1) * P], ident[:, :])
                last.then_inc(wo_turned, 1)
                pe.wait_ge(qk_lo_ready, 2)
                pe.wait_ge(wo_centred, 2)

            def fold_weights():
                for j in range(CH):
                    last = pe.matmul(z_sum[:, j * 2 * P:(j + 1) * 2 * P], wv_raw[:, j, :], wo_pairs[:, j, :, :],
                                     start=True, stop=True)
                last.then_inc(z_folded, 1)

            def keys(s, par, i, edge):
                wait_slot(pe, f"K{i}", s, edge)
                if i == 0:
                    pe.wait_ge(ctx_lo_ready, s + 1)
                out = slot(f"K{i}")
                for n in range(2):
                    c = slice(n * BANK, (n + 1) * BANK)
                    last = split_products(pe, out[:, n], wk_hi[:, i * P:(i + 1) * P], wk_lo[:, i * P:(i + 1) * P],
                                          ctx_hi[:, par, c], ctx_lo[:, par, c], True, True)
                last.then_inc(k_made, 1)

            def queries(s, par, i, edge):
                wait_slot(pe, f"Q{i}", s, edge)
                if i == 0:
                    pe.wait_ge(xn_lo_ready, s + 1)
                out = slot(f"Q{i}")
                for n in range(2):
                    c = slice((2 * i + n) * P, (2 * i + n + 1) * P)
                    last = split_products(pe, out[:, n], xn_hi[:, par, c], xn_lo[:, par, c],
                                          wq_hi[:, :], wq_lo[:, :], True, True)
                last.then_inc(q_made, 1)

            def turn_query(s, par, j, edge):
                wait_slot(pe, f"QT{j}", s, edge)
                pe.wait_ge(q_normed, 4 * (s - 1) + 4)
                out = flat(f"QT{j}")
                for n in range(NCH):
                    last = pe.transpose(out[:, n * P:(n + 1) * P], eq[:, 1 - par, n, j * P:(j + 1) * P], ident[:, :])
                last.then_inc(q_turned, 1)

            def turn_keys(s, par, i, edge):
                wait_slot(pe, f"KT{i}", s, edge)
                pe.wait_ge(k_exp, 4 * (s - 1) + 4)
                out = slot(f"KT{i}")
                for n in range(2):
                    for j in range(CH):
                        c = (2 * i + n) * P
                        last = pe.transpose(out[:, n, j * P:(j + 1) * P], ek[:, 1 - par, j, c:c + P], ident[:, :])
                last.then_inc(kT_turned, 1)

            def turn_context(s, par, edge):
                wait_slot(pe, "C0", s, edge)
                pe.wait_ge(ctx_loaded[par], 8 * (s - par) + 16)
                out = flat("C0")
                for n in range(NCH):
                    last = pe.transpose(out[:, n * P:(n + 1) * P], ctx_sb[:, par, n * P:(n + 1) * P], ident[:, :])
                last.then_inc(c_turned, 1)

            def add_output(b, j):
                pe.wait_ge(q_lo_ready, 4 * b + j + 1)
                if j == 0:
                    pe.wait_ge(m_lo_ready, b + 1)
                    pe.wait_ge(t_lo_ready, b + 1)
                for n in range(2):
                    c = slice(n * BANK, (n + 1) * BANK)
                    last = split_products(pe, acc[:, n], m_hi[:, j, :], m_lo[:, j, :], q_hi[:, j % 2, c],
                                          q_lo[:, j % 2, c], j == 0, j == CH - 1)
                last.then_inc(o_part, 1)

            def add_weighted(b, i):
                pe.wait_ge(kT_lo_ready, 4 * b + i + 1)
                if i == 0:
                    if isinstance(b, int) and b == 0:
                        pe.wait_ge(z_lo_ready, 1)
                    pe.wait_ge(cT_lo_ready, b + 1)
                    wait_for(pe, o_copied, b)
                for n in range(2):
                    last = split_products(pe, acc[:, 0], cT_hi[:, 2 * i + n, :], cT_lo[:, 2 * i + n, :],
                                          kT_hi[:, i % 2, n, :], kT_lo[:, i % 2, n, :],
                                          i == 0 and n == 0, i == CH - 1 and n == 1)
                last.then_inc(t_part, 1)

            def fold(s, edge):
                wait_slot(pe, "M0", s, edge)
                pe.wait_ge(t_lo_ready, s - 1 + 1)
                for j in range(CH):
                    out = flat("M0")[:, 2 * j * P:2 * (j + 1) * P]
                    c, z = slice(j * P, (j + 1) * P), slice(2 * j * P, 2 * (j + 1) * P)
                    last = split_products(pe, out, t_hi[:, c], t_lo[:, c], z_hi[:, z], z_lo[:, z], True, True)
                last.then_inc(m_made, 1)

            def step(s, par, edge):
                X_, K, Q, C, KT, M, QT, O = (on(k, s, edge) for k in STAGES)
                if edge and s == 0:
                    turn_weights()
                if edge and s == 1:
                    fold_weights()
                if KT:
                    turn_keys(s, par, 0, edge)
                if Q:
                    queries(s, par, 0, edge)
                if KT:
                    turn_keys(s, par, 1, edge)
                if O:
                    add_output(s - 2, 3)
                if K:
                    keys(s, par, 0, edge)
                if KT:
                    turn_keys(s, par, 2, edge)
                if Q:
                    queries(s, par, 1, edge)
                if KT:
                    add_weighted(s - 1, 0)
                    turn_keys(s, par, 3, edge)
                    add_weighted(s - 1, 1)
                if K:
                    keys(s, par, 1, edge)
                if Q:
                    queries(s, par, 2, edge)
                if QT:
                    turn_query(s, par, 0, edge)
                if KT:
                    add_weighted(s - 1, 2)
                    add_weighted(s - 1, 3)
                if K:
                    keys(s, par, 2, edge)
                if M:
                    fold(s, edge)
                if QT:
                    turn_query(s, par, 1, edge)
                if Q:
                    queries(s, par, 3, edge)
                if QT:
                    turn_query(s, par, 2, edge)
                    add_output(s - 1, 0)
                if K:
                    keys(s, par, 3, edge)
                if QT:
                    add_output(s - 1, 1)
                    turn_query(s, par, 3, edge)
                if C:
                    turn_context(s, par, edge)
                if QT:
                    add_output(s - 1, 2)

            each_step(pe, step)


GROUPS = ((0, EXPERTS + 2 * P), (EXPERTS + 2 * P, EXPERTS + 5 * P), (EXPERTS + 5 * P, EXPERTS + 8 * P))
A_JOBS = 1 + KCH
WEIGHT_JOBS = A_JOBS + KCH


def expert_mix(nc, ident, ps, w, shared, x, o_dram, A, B, out):
    with ExitStack() as ctx:
        def sb(name, shape, dt=F32):
            return ctx.enter_context(nc.sbuf_tensor(name, shape, dt))

        def sem(name):
            return ctx.enter_context(nc.semaphore(name))

        ORDERED = 3
        ra = [sb(f"w_ra_{part}", [P, NCH, EXPERTS + KR], F32R) for part in ("hi", "lo")]
        wb = [sb(f"w_b_{part}", [P, KCH, N], F32R) for part in ("hi", "lo")]
        (ra_hi, ra_lo), (b_hi, b_lo) = ra, wb
        b_rows = sb("b_rows", [P, ORDERED, NCH, P])

        x_sb, o_sb, o_stored = shared["x_sb"], shared["o_sb"], shared["o_stored"]
        x2 = sb("x2", [P, 2, N])
        out_sb = sb("out_sb", [P, N])
        work = sb("work", [P, N])
        xT_hi = sb("xT_hi", [P, NCH, P], F32R)
        xT_lo = sb("xT_lo", [P, NCH, P], F32R)
        hg = sb("hg", [P, KR])
        hT_hi = sb("hT_hi", [P, KCH, P], F32R)
        hT_lo = sb("hT_lo", [P, KCH, P], F32R)
        var_c = sb("var_c", [P, NCH])
        rstd_c = sb("rstd_c", [P, NCH])
        stats = sb("stats2", [P, 2, 6])
        mv = sb("mv2", [P, 2])
        veps = sb("veps2", [P, 1])
        rstd = sb("rstd2", [P, 1])
        shift = sb("shift2", [P, 1])
        score = sb("score", [P, EXPERTS])
        top = sb("top", [P, 2, 8])
        neg_top = sb("neg_top", [P, 1])
        rest = sb("rest", [P, 2, EXPERTS])
        e_all = sb("e_all", [P, EXPERTS])
        e_rest = sb("e_rest", [P, EXPERTS])
        gate_sum = sb("gate_sum", [P, 1])
        gate_inv = sb("gate_inv", [P, 1])
        gate_raw = sb("gate_raw", [P, EXPERTS])
        gate = sb("gate", [P, EXPERTS])
        raw = [x_sb[:, 1, :], x2[:, 1, :], o_sb[:, 1, :], out_sb[:, :]]
        RAW = len(raw)

        raw_loaded = shared["raw_loaded"] + [sem(f"raw_loaded{i}") for i in range(1, RAW)]
        b_ordered = [sem(f"b_ordered{i}") for i in range(2)]
        w_turned, w_hi_ready, w_lo_ready = sem("w_turned"), sem("w_hi_ready"), sem("w_lo_ready")
        x_loaded, o_loaded = shared["x_loaded"], shared["o_loaded"]
        stored = sem("stored")
        o_turned, y_turned, x_turned = sem("o_turned"), sem("y_turned"), sem("x_turned")
        h_made, h_turned, r_made = sem("h_made"), sem("h_turned"), sem("r_made")
        squared, xn_ready, x_hi_ready, h_hi_ready = sem("squared"), sem("xn2_ready"), sem("x_hi_ready"), sem("h_hi_ready")
        scores_copied, e_all_ready, e_rest_ready = sem("scores_copied"), sem("e_all_ready"), sem("e_rest_ready")
        var_sum, var_ready, y_ready, x2_ready = sem("var_sum"), sem("var_ready"), sem("y_ready"), sem("x2_ready")
        x2_stats, x2_mean, veps_ready, shift_ready = sem("x2_stats"), sem("x2_mean"), sem("veps2_ready"), sem("shift_ready2")
        rstd_c_ready, rstd_ready = sem("rstd_c_ready"), sem("rstd2_ready")
        x_lo_ready, h_lo_ready, h_gated, added = sem("x_lo_ready"), sem("h_lo_ready"), sem("h_gated"), sem("added")
        top_step, neg_top_ready, gate_step, gates_ready = sem("top_step"), sem("neg_top_ready"), sem("gate_step"), sem("gates_ready")

        OT = YT = XT = ps[:, 0]
        HT = ps[:, 1, 0]
        H = [ps[:, 2, 0], ps[:, 2, 1], ps[:, 1, 1]]
        R = ps[:, 3]
        flat = "p a b -> p (a b)"

        def weight_slot(n):
            pair = ((2, 3, 1) if n < A_JOBS else (0, 3, 1))[n % 3]
            width = EXPERTS if n == 0 else P
            return ps[:, pair].rearrange("p a (b c) -> p (a b) c", c=P)[:, :, 0:width]

        def weight_part(i, n):
            if n == 0:
                return ra[i][:, :, 0:EXPERTS]
            if n < A_JOBS:
                return ra[i][:, :, EXPERTS + (n - 1) * P:EXPERTS + n * P]
            return wb[i][:, n - A_JOBS, :].rearrange("q (p j) -> q j p", j=NCH)

        def weight_jobs(t, place):
            return {(-1, "var"): range(0, 2), (-1, "o"): range(2, 4), (-1, "y"): range(4, 6),
                    (-1, "norm"): range(6, 7), (-1, "x"): range(7, A_JOBS),
                    (0, "start"): range(A_JOBS, A_JOBS + 3),
                    (0, "scores"): range(A_JOBS + 3, WEIGHT_JOBS)}.get((t, place), ()) if isinstance(t, int) else ()

        def order_rows(eng, op, m):
            n = A_JOBS + m
            eng.wait_ge(raw_loaded[n % RAW], 16 * (n // RAW + 1))
            if m >= ORDERED:
                eng.wait_ge(w_turned, n - ORDERED + 1)
            op(b_rows[:, m % ORDERED, :, :].rearrange("p j (k r) -> p k j r", k=8),
               raw[n % RAW].rearrange("p (k j r) -> p k j r", k=8, j=NCH)).then_inc(b_ordered[m % 2], 1)

        def each_step(eng, step):
            for t in (-1, 0, 1, 2):
                step(t, t % 2, t >= 0, True, t >= 1)
            with eng.Fori(0, (BATCHES - 4) // 2) as i:
                for k in range(2):
                    step(2 * i + 3 + k, (3 + k) % 2, True, True, True)
            step(BATCHES - 1, (BATCHES - 1) % 2, True, False, True)
            step(BATCHES, BATCHES % 2, False, False, True)

        block = ctx.enter_context(nc.Block())

        @block.sync
        def _(sp):
            def load(b, p):
                wait_for(sp, o_turned, b - 1)
                if isinstance(b, int) and b == 1:
                    sp.wait_ge(b_ordered[1], KCH // 2 - 1)
                sp.dma_start(o_sb[:, p, :], o_dram[b]).then_inc(o_loaded[p], 16)
                wait_for(sp, x2_ready, b - 1)
                if isinstance(b, int) and b == 1:
                    sp.wait_ge(b_ordered[1], KCH // 2)
                sp.dma_start(x_sb[:, p, :], x[b]).then_inc(x_loaded[p], 16)

            def load_weights():
                a_v = A.rearrange("k r d -> (k r) d")
                for n in range(1, WEIGHT_JOBS):
                    before = n - RAW
                    if 0 <= before < A_JOBS:
                        sp.wait_ge(w_turned, before + 1)
                    elif before >= A_JOBS:
                        m = before - A_JOBS
                        sp.wait_ge(b_ordered[m % 2], m // 2 + 1)
                    if n == 2:
                        sp.wait_ge(o_stored[1], 16 * BATCHES // 2)
                    if n < A_JOBS:
                        dst, src = raw[n % RAW], a_v[(n - 1) * P:n * P, :]
                    else:
                        m = n - A_JOBS
                        dst = raw[n % RAW].rearrange("p (k m) -> p k m", k=8)
                        src = B[m * 8:(m + 1) * 8].rearrange("k (p j) r -> p k (j r)", j=NCH)
                    sp.dma_start(dst, src).then_inc(raw_loaded[n % RAW], 16)

            def step(t, par, mix, ahead, tail):
                if ahead and (not isinstance(t, int) or t + 2 < BATCHES):
                    load(t + 2, par)
                if tail:
                    sp.wait_ge(added, t)
                    sp.dma_start(out[t - 1], out_sb[:, :]).then_inc(stored, 16)

            load_weights()
            for t in (-1, 0, 1, 2):
                step(t, t % 2, t >= 0, True, t >= 1)
            with sp.Fori(0, (BATCHES - 4) // 2 - 1) as i:
                for k in range(2):
                    step(2 * i + 3 + k, (3 + k) % 2, True, True, True)
            for t in range(BATCHES - 3, BATCHES + 1):
                step(t, t % 2, True, t < BATCHES - 1, True)
            sp.wait_ge(stored, 16 * BATCHES)

        @block.gpsimd
        def _(pool):
            def step(t, par, mix, ahead, tail):
                if ahead:
                    b = t + 1
                    pool.wait_ge(var_ready, b + 1)
                    wait_for(pool, y_ready, b)
                    pool.tensor_tensor(rstd_c[:, :], var_c[:, :], w["minus_half"][:, 0:1].broadcast_to([P, NCH]),
                                       ALU.pow).then_inc(rstd_c_ready, 1)
                    pool.wait_ge(veps_ready, b + 1)
                    wait_for(pool, xn_ready, b)
                    pool.tensor_tensor(rstd[:, :], veps[:, :], w["minus_half"][:, :], ALU.pow).then_inc(rstd_ready, 1)

            each_step(pool, step)

        @block.scalar
        def _(act):
            def weights(t, place):
                for n in weight_jobs(t, place):
                    m = n - A_JOBS
                    if m >= 0 and m % 2 == 0 and m + 2 < KCH:
                        order_rows(act, act.copy, m + 2)
                    act.wait_ge(w_turned, n + 1)
                    act.copy(weight_part(0, n), weight_slot(n)).then_inc(w_hi_ready, 1)

            def turned_hidden(t, half):
                act.wait_ge(h_turned, 2 * t + half + 1)
                wait_for(act, r_made, t)
                dst = hT_hi[:, half * 4:half * 4 + 4, :].rearrange(flat)
                act.copy(dst, HT).then_inc(h_hi_ready, 1)

            def step(t, par, mix, ahead, tail):
                b = t + 1
                weights(t, "start")
                weights(t, "scores")
                if mix:
                    act.wait_ge(neg_top_ready, t + 1)
                    wait_for(act, gate_step, 3 * t)
                    act.activation(e_all[:, :], score[:, :], ACT.Exp, bias=neg_top[:, 0:1],
                                   scale=1.0).then_inc(e_all_ready, 1)
                if ahead:
                    act.wait_ge(o_turned, b + 1)
                    wait_for(act, x_turned, b)
                    act.activation(work[:, :], OT.rearrange(flat), ACT.Square).then_inc(squared, 1)
                if mix:
                    act.wait_ge(top_step, 2 * t + 2)
                    wait_for(act, gate_step, 3 * t)
                    act.activation(e_rest[:, :], rest[:, 1, :], ACT.Exp, bias=neg_top[:, 0:1],
                                   scale=1.0).then_inc(e_rest_ready, 1)
                weights(t, "var")
                weights(t, "o")
                weights(t, "y")
                if mix:
                    turned_hidden(t, 0)
                if ahead:
                    act.wait_ge(shift_ready, b + 1)
                    act.wait_ge(y_turned, b + 1)
                    act.activation(work[:, :], x2[:, 1 - par, :], ACT.Identity, bias=shift[:, 0:1],
                                   scale=rstd[:, 0:1]).then_inc(xn_ready, 1)
                weights(t, "norm")
                if not mix and ahead:
                    order_rows(act, act.copy, 0)
                if ahead:
                    act.wait_ge(x_turned, b + 1)
                    wait_for(act, h_made, 3 * b)
                    act.copy(xT_hi[:, :, :].rearrange(flat), XT.rearrange(flat)).then_inc(x_hi_ready, 1)
                weights(t, "x")
                if mix:
                    turned_hidden(t, 1)

            each_step(act, step)

        @block.vector
        def _(dve):
            def weights(t, place):
                for n in weight_jobs(t, place):
                    m = n - A_JOBS
                    if m >= 0 and m % 2 == 1 and m + 2 < KCH:
                        order_rows(dve, dve.tensor_copy, m + 2)
                    dve.wait_ge(w_hi_ready, n + 1)
                    dve.tensor_tensor(weight_part(1, n), weight_slot(n), weight_part(0, n).bitcast(F32),
                                      ALU.subtract).then_inc(w_lo_ready, 1)

            def gate_hidden(t, g):
                dve.wait_ge(h_made, 3 * t + g + 1)
                if g == 0:
                    dve.wait_ge(gates_ready, t + 1)
                wait_for(dve, h_turned, 2 * t - 1 if g == 0 else 2 * t)
                lo, hi = (max(c - EXPERTS, 0) for c in GROUPS[g])
                k0, k1 = lo // RANK, hi // RANK
                c0 = EXPERTS if g == 0 else 0
                dve.tensor_tensor(hg[:, lo:hi].rearrange("p (k r) -> p k r", r=RANK),
                                  H[g][:, c0:c0 + hi - lo].rearrange("p (k r) -> p k r", r=RANK),
                                  per_row(gate[:, k0:k1], k1 - k0, RANK), ALU.mult).then_inc(h_gated, 1)

            def turned_hidden(t, half):
                dve.wait_ge(h_hi_ready, 2 * t + half + 1)
                c = slice(half * 4, half * 4 + 4)
                dve.tensor_tensor(hT_lo[:, c, :].rearrange(flat), HT, hT_hi[:, c, :].rearrange(flat).bitcast(F32),
                                  ALU.subtract).then_inc(h_lo_ready, 1)

            def top_scores(t):
                dve.wait_ge(h_made, 3 * t + 1)
                wait_for(dve, e_all_ready, t)
                dve.tensor_copy(score[:, :], H[0][:, 0:EXPERTS]).then_inc(scores_copied, 1)
                dve.drain()
                dve.max(top[:, 0, :], score[:, :]).then_inc(top_step, 1)
                dve.wait_ge(top_step, 2 * t + 1)
                wait_for(dve, e_rest_ready, t)
                dve.tensor_scalar(neg_top[:, :], top[:, 0, 0:1], -1.0, None, ALU.mult).then_inc(neg_top_ready, 1)
                dve.match_replace(rest[:, 0, :], top[:, 0, :], score[:, :], LOWEST)
                dve.drain()
                dve.max(top[:, 1, :], rest[:, 0, :])
                dve.drain()
                dve.match_replace(rest[:, 1, :], top[:, 1, :], rest[:, 0, :], LOWEST).then_inc(top_step, 1)

            def gates(t):
                dve.wait_ge(e_all_ready, t + 1)
                dve.wait_ge(e_rest_ready, t + 1)
                dve.tensor_tensor(gate_raw[:, :], e_all[:, :], e_rest[:, :], ALU.subtract).then_inc(gate_step, 1)
                dve.wait_ge(gate_step, 3 * t + 1)
                dve.tensor_reduce(gate_sum[:, :], gate_raw[:, :], X, ALU.add).then_inc(gate_step, 1)
                dve.wait_ge(gate_step, 3 * t + 2)
                dve.reciprocal(gate_inv[:, :], gate_sum[:, :]).then_inc(gate_step, 1)
                dve.wait_ge(gate_step, 3 * t + 3)
                dve.tensor_scalar(gate[:, :], gate_raw[:, :], gate_inv[:, 0:1], MIX_SCALE, ALU.mult,
                                  ALU.mult).then_inc(gates_ready, 1)

            def step(t, par, mix, ahead, tail):
                b, p = t + 1, 1 - par
                weights(t, "start")
                weights(t, "scores")
                if mix:
                    top_scores(t)
                if ahead:
                    dve.wait_ge(squared, b + 1)
                    dve.tensor_reduce(var_c[:, :], work[:, :].rearrange("p (n c) -> p n c", c=P), X,
                                      ALU.add).then_inc(var_sum, 1)
                    dve.wait_ge(var_sum, b + 1)
                    dve.tensor_scalar(var_c[:, :], var_c[:, :], 1.0 / P, EPS, ALU.mult, ALU.add).then_inc(var_ready, 1)
                weights(t, "var")
                if mix:
                    gates(t)
                if ahead:
                    dve.wait_ge(rstd_c_ready, b + 1)
                    dve.tensor_tensor(work[:, :].rearrange("p (n c) -> p n c", c=P),
                                      OT.rearrange("p a (b c) -> p (a b) c", c=P), per_row(rstd_c[:, :], NCH, P),
                                      ALU.mult).then_inc(y_ready, 1)
                if mix:
                    gate_hidden(t, 0)
                weights(t, "o")
                if tail:
                    dve.wait_ge(r_made, t)
                    wait_for(dve, stored, 16 * (t - 1))
                    dve.tensor_tensor(out_sb[:, :], R.rearrange(flat), x2[:, 1 - par, :], ALU.add).then_inc(added, 1)
                if ahead:
                    dve.wait_ge(y_turned, b + 1)
                    dve.wait_ge(x_loaded[p], 8 * (b - p) + 16)
                    wait_for(dve, xn_ready, b - 1)
                    wait_for(dve, added, b - 1)
                    dve.scalar_tensor_tensor(out=x2[:, p, :], in0=YT.rearrange(flat), scalar=w["g"][:, 0:1],
                                             in1=x_sb[:, p, :], op0=ALU.mult, op1=ALU.add).then_inc(x2_ready, 1)
                    dve.wait_ge(x2_ready, b + 1)
                    for h in range(2):
                        dve.bn_stats(stats[:, h, :], x2[:, p, h * BANK:(h + 1) * BANK]).then_inc(x2_stats, 1)
                if mix:
                    gate_hidden(t, 1)
                if ahead:
                    dve.drain()
                    dve.bn_aggr(mv[:, :], stats[:, :, :]).then_inc(x2_mean, 1)
                    dve.wait_ge(x2_mean, b + 1)
                    dve.tensor_scalar(veps[:, :], mv[:, 1:2], EPS, None, ALU.add).then_inc(veps_ready, 1)
                    dve.wait_ge(rstd_ready, b + 1)
                    dve.scalar_tensor_tensor(out=shift[:, :], in0=mv[:, 0:1], scalar=-1.0, in1=rstd[:, :],
                                             op0=ALU.mult, op1=ALU.mult).then_inc(shift_ready, 1)
                weights(t, "y")
                weights(t, "norm")
                if not mix and ahead:
                    order_rows(dve, dve.tensor_copy, 1)
                if mix:
                    turned_hidden(t, 0)
                    gate_hidden(t, 2)
                if ahead:
                    dve.wait_ge(x_hi_ready, b + 1)
                    dve.tensor_tensor(xT_lo[:, :, :].rearrange(flat), XT.rearrange(flat),
                                      xT_hi[:, :, :].rearrange(flat).bitcast(F32), ALU.subtract).then_inc(x_lo_ready, 1)
                weights(t, "x")
                if mix:
                    turned_hidden(t, 1)

            each_step(dve, step)

        @block.tensor
        def _(pe):
            def turn(dst, src, done):
                for n in range(src.shape[1] // P):
                    last = pe.transpose(dst[:, n * P:(n + 1) * P], src[:, n * P:(n + 1) * P], ident[:, :])
                last.then_inc(done, 1)

            def weights(t, place):
                for n in weight_jobs(t, place):
                    m = n - A_JOBS
                    if m >= 0:
                        pe.wait_ge(b_ordered[m % 2], m // 2 + 1)
                    else:
                        pe.wait_ge(raw_loaded[n % RAW], 16 * (n // RAW + 1))
                    if n >= 3:
                        pe.wait_ge(w_lo_ready, n - 2)
                    rows = slice(0, EXPERTS if n == 0 else P)
                    for j in range(NCH):
                        src = b_rows[:, m % ORDERED, j, :] if m >= 0 else raw[n % RAW][rows, j * P:(j + 1) * P]
                        last = pe.transpose(weight_slot(n)[:, j, :], src, ident[rows, rows])
                    last.then_inc(w_turned, 1)

            def hidden(g, chunks):
                c0, c1 = GROUPS[g]
                for n in chunks:
                    last = split_products(pe, H[g][:, 0:c1 - c0], xT_hi[:, n, :], xT_lo[:, n, :],
                                          ra_hi[:, n, c0:c1], ra_lo[:, n, c0:c1], n == 0, n == NCH - 1)
                return last

            def result(chunks):
                for q in chunks:
                    for d in range(2):
                        last = split_products(pe, R[:, d], hT_hi[:, q, :], hT_lo[:, q, :],
                                              b_hi[:, q, d * BANK:(d + 1) * BANK],
                                              b_lo[:, q, d * BANK:(d + 1) * BANK], q == 0, q == KCH - 1)
                return last

            def step(t, par, mix, ahead, tail):
                b, p = t + 1, 1 - par
                if mix:
                    if isinstance(t, int) and t == 0:
                        pe.wait_ge(w_lo_ready, A_JOBS)
                    pe.wait_ge(x_lo_ready, t + 1)
                    weights(t, "start")
                    wait_for(pe, h_gated, 3 * (t - 1) + 1)
                    hidden(0, range(NCH)).then_inc(h_made, 1)
                weights(t, "scores")
                if isinstance(t, int) and t == 0:
                    pe.wait_ge(w_lo_ready, WEIGHT_JOBS - 1)
                if ahead:
                    pe.wait_ge(o_loaded[p], 8 * (b - p) + 16)
                    if not mix:
                        wait_for(pe, x_lo_ready, b)
                    turn(OT.rearrange(flat), o_sb[:, p, :], o_turned)
                weights(t, "var")
                weights(t, "o")
                if tail:
                    pe.wait_ge(h_lo_ready, 2 * t)
                    result(range(KCH // 2, KCH)).then_inc(r_made, 1)
                if mix:
                    wait_for(pe, h_gated, 3 * (t - 1) + 2)
                    hidden(1, range(NCH // 2))
                if ahead:
                    pe.wait_ge(y_ready, b + 1)
                    turn(YT.rearrange(flat), work[:, :], y_turned)
                weights(t, "y")
                weights(t, "norm")
                if mix:
                    hidden(1, range(NCH // 2, NCH)).then_inc(h_made, 1)
                    wait_for(pe, h_gated, 3 * (t - 1) + 3)
                    hidden(2, range(NCH // 2))
                    pe.wait_ge(h_gated, 3 * t + 2)
                    wait_for(pe, h_lo_ready, 2 * t)
                    turn(HT, hg[:, 0:BANK], h_turned)
                    hidden(2, range(NCH // 2, NCH)).then_inc(h_made, 1)
                    pe.wait_ge(h_lo_ready, 2 * t + 1)
                    wait_for(pe, added, t)
                    if isinstance(t, int) and t == 0:
                        pe.wait_ge(w_lo_ready, WEIGHT_JOBS)
                    result(range(1))
                if ahead:
                    pe.wait_ge(xn_ready, b + 1)
                    pe.wait_ge(x2_ready, b + 1)
                    turn(XT.rearrange(flat), work[:, :], x_turned)
                weights(t, "x")
                if mix:
                    pe.wait_ge(h_gated, 3 * t + 3)
                    turn(HT, hg[:, BANK:2 * BANK], h_turned)
                    result(range(1, KCH // 2))

            each_step(pe, step)


def xattn_ffn(nc, x, context, Wq, Wkv, Wout, b_out, g, A, B, Wr, out):
    o_dram = nc.dram_tensor("attention_out", (BATCHES, P, N), F32).ap()
    with ExitStack() as ctx:
        def sb(name, shape, dt=F32):
            return ctx.enter_context(nc.sbuf_tensor(name, shape, dt))

        ps = ctx.enter_context(nc.psum_tensor("ps", [P, 4, 2, BANK], F32))
        ident = sb("ident", [P, P])
        w = {"g": sb("g_col", [P, 1]), "bias": sb("bias_col", [P, 1]), "minus_half": sb("minus_half", [P, 1]),
             "one": sb("one", [P, 1])}
        shared = {"x_sb": sb("x_sb", [P, 2, N]), "o_sb": sb("o_sb", [P, 2, N])}
        for name, count in (("o_stored", 2), ("x_loaded", 2), ("o_loaded", 2), ("raw_loaded", 1)):
            shared[name] = [ctx.enter_context(nc.semaphore(f"mix_{name}{i}")) for i in range(count)]
        attention(nc, ident, ps, w, shared, x, context, Wq, Wkv, Wout, b_out, g, Wr, o_dram)
        expert_mix(nc, ident, ps, w, shared, x, o_dram, A, B, out)


_INS = ["x", "ctx_4096", "L0_xattn_Wq", "L0_xattn_Wkv", "L0_xattn_Wout", "L0_xattn_b_out", "L0_xattn_g",
        "L0_ffn_A", "L0_ffn_B", "L0_ffn_Wr"]


def kernel(**inputs):
    import numpy as _np
    import concourse.bacc as _bacc
    from concourse import mybir as _mybir
    from concourse.bass_utils import run_bass_kernel_spmd as _run

    nc = _bacc.Bacc("TRN2", target_bir_lowering=False, num_devices=1)
    arrays, args = {}, []
    for name in _INS:
        a = _np.ascontiguousarray(inputs[name])
        arrays[f"in_{name}"] = a
        args.append(nc.dram_tensor(f"in_{name}", a.shape, _mybir.dt.from_np(a.dtype), kind="ExternalInput").ap())
    args.append(nc.dram_tensor("out_0", (BATCHES, P, N), F32, kind="ExternalOutput").ap())
    xattn_ffn(nc, *args)
    r = _run(nc, [arrays], core_ids=[0])
    return r.results[0]["out_0"]
```
